# Optimizing a Trainium2 kernel written in Bass

```python
import numpy as np
import jax
import jax.numpy as jnp

def _softmax(x, axis=-1):
    return jax.nn.softmax(x, axis=axis)

def _gelu(x):
    return jax.nn.gelu(x, approximate=True)

def _silu(x):
    return jax.nn.silu(x)

def _sigmoid(x):
    return jax.nn.sigmoid(x)

def _layernorm(x, axis=-1, eps=1e-05):
    m = jnp.mean(x, axis=axis, keepdims=True)
    v = jnp.var(x, axis=axis, keepdims=True)
    return (x - m) / jnp.sqrt(v + eps)

def _scatter_add(tgt, idx, src, axis=0):
    return tgt.at[idx].add(src)

def _segment_sum(src, seg, n):
    return jax.ops.segment_sum(src, seg, n)
kernel_name = 'mk_macaron_d1_jaxref_r4_67c260'

def setup_inputs(seed: int=0):
    np.random.seed(seed)
    _w = jnp.asarray

    def _L0_attn_setup():
        import jax, jax.numpy as jnp
        import numpy as np
        B, S, D, DI = (2, 1024, 256, 1024)

        def _gelu(x):
            return jax.nn.gelu(x, approximate=False)

        def _ln(x, g, b, eps=1e-05):
            mu = jnp.mean(x, axis=-1, keepdims=True)
            var = jnp.mean((x - mu) ** 2, axis=-1, keepdims=True)
            return (x - mu) / jnp.sqrt(var + eps) * g + b

        def _mlp(x, w1, b1, w2, b2):
            return _gelu(x @ w1 + b1) @ w2 + b2
        key = jax.random.key(seed)
        ks = jax.random.split(key, 16)
        s = 0.02

        def W(k, shape):
            return jax.random.normal(k, shape, dtype=jnp.float32) * s
        return {'x': jax.random.normal(ks[0], (B, S, D), dtype=jnp.float32), 'ln_g': jnp.ones((D,), jnp.float32), 'ln_b': jnp.zeros((D,), jnp.float32), 'h1_w1': W(ks[1], (D, DI)), 'h1_b1': jnp.zeros((DI,), jnp.float32), 'h1_w2': W(ks[2], (DI, D)), 'h1_b2': jnp.zeros((D,), jnp.float32), 'h2_w1': W(ks[3], (D, DI)), 'h2_b1': jnp.zeros((DI,), jnp.float32), 'h2_w2': W(ks[4], (DI, D)), 'h2_b2': jnp.zeros((D,), jnp.float32), 'fm_w1': W(ks[5], (D, DI)), 'fm_b1': jnp.zeros((DI,), jnp.float32), 'fm_w2': W(ks[6], (DI, D)), 'fm_b2': jnp.zeros((D,), jnp.float32)}
    _L0_attn_in = _L0_attn_setup()

    def _L0_ffn_setup():
        import jax, jax.numpy as jnp
        import numpy as np
        H = 256
        I = 128
        E = 64
        K = 2
        EPS = 1e-06
        CAP = 256

        def _rmsnorm(x, w, eps=EPS):
            v = jnp.mean(x.astype(jnp.float32) ** 2, axis=-1, keepdims=True)
            return (x.astype(jnp.float32) * jax.lax.rsqrt(v + eps)).astype(x.dtype) * w
        key = jax.random.key(seed)
        ks = jax.random.split(key, 8)
        B, S = (2, 1024)
        s_h = 1.0 / np.sqrt(H)
        s_i = 1.0 / np.sqrt(I)
        return {'hidden_states': jax.random.normal(ks[0], (B, S, H), jnp.float32), 'rms_w': jnp.ones((H,), jnp.float32), 'gate_w': jax.random.normal(ks[1], (E, H), jnp.float32) * s_h, 'w13': jax.random.normal(ks[2], (E, H, 2 * I), jnp.float32) * s_h, 'w2': jax.random.normal(ks[3], (E, I, H), jnp.float32) * s_i, 'sw_gate': jax.random.normal(ks[4], (H, I), jnp.float32) * s_h, 'sw_up': jax.random.normal(ks[5], (H, I), jnp.float32) * s_h, 'sw_down': jax.random.normal(ks[6], (I, H), jnp.float32) * s_i}
    _L0_ffn_in = _L0_ffn_setup()
    _d = {'L0_attn_x': _L0_attn_in['x'], 'L0_attn_ln_g': _L0_attn_in['ln_g'], 'L0_attn_ln_b': _L0_attn_in['ln_b'], 'L0_attn_h1_w1': _L0_attn_in['h1_w1'], 'L0_attn_h1_b1': _L0_attn_in['h1_b1'], 'L0_attn_h1_w2': _L0_attn_in['h1_w2'], 'L0_attn_h1_b2': _L0_attn_in['h1_b2'], 'L0_attn_h2_w1': _L0_attn_in['h2_w1'], 'L0_attn_h2_b1': _L0_attn_in['h2_b1'], 'L0_attn_h2_w2': _L0_attn_in['h2_w2'], 'L0_attn_h2_b2': _L0_attn_in['h2_b2'], 'L0_attn_fm_w1': _L0_attn_in['fm_w1'], 'L0_attn_fm_b1': _L0_attn_in['fm_b1'], 'L0_attn_fm_w2': _L0_attn_in['fm_w2'], 'L0_attn_fm_b2': _L0_attn_in['fm_b2'], 'L0_ffn_rms_w': _L0_ffn_in['rms_w'], 'L0_ffn_gate_w': _L0_ffn_in['gate_w'], 'L0_ffn_w13': _L0_ffn_in['w13'], 'L0_ffn_w2': _L0_ffn_in['w2'], 'L0_ffn_sw_gate': _L0_ffn_in['sw_gate'], 'L0_ffn_sw_up': _L0_ffn_in['sw_up'], 'L0_ffn_sw_down': _L0_ffn_in['sw_down']}
    _x0 = _d['L0_attn_x']
    _d['L0_attn_x'] = jax.random.normal(jax.random.fold_in(jax.random.key(seed), 1), (8, 1024, 256), dtype=_x0.dtype)
    del _x0
    return _d

def reference(L0_attn_x, L0_attn_ln_g, L0_attn_ln_b, L0_attn_h1_w1, L0_attn_h1_b1, L0_attn_h1_w2, L0_attn_h1_b2, L0_attn_h2_w1, L0_attn_h2_b1, L0_attn_h2_w2, L0_attn_h2_b2, L0_attn_fm_w1, L0_attn_fm_b1, L0_attn_fm_w2, L0_attn_fm_b2, L0_ffn_rms_w, L0_ffn_gate_w, L0_ffn_w13, L0_ffn_w2, L0_ffn_sw_gate, L0_ffn_sw_up, L0_ffn_sw_down):

    def _L0_attn_ref(x, ln_g, ln_b, h1_w1, h1_b1, h1_w2, h1_b2, h2_w1, h2_b1, h2_w2, h2_b2, fm_w1, fm_b1, fm_w2, fm_b2):
        import jax, jax.numpy as jnp
        import numpy as np
        B, S, D, DI = (2, 1024, 256, 1024)

        def _gelu(x):
            return jax.nn.gelu(x, approximate=False)

        def _ln(x, g, b, eps=1e-05):
            mu = jnp.mean(x, axis=-1, keepdims=True)
            var = jnp.mean((x - mu) ** 2, axis=-1, keepdims=True)
            return (x - mu) / jnp.sqrt(var + eps) * g + b

        def _mlp(x, w1, b1, w2, b2):
            return _gelu(x @ w1 + b1) @ w2 + b2
        n = _ln(x, ln_g, ln_b)
        W1 = _mlp(n, h1_w1, h1_b1, h1_w2, h1_b2)
        W2 = _mlp(n, h2_w1, h2_b1, h2_w2, h2_b2)
        W3 = jnp.einsum('bzn,bsn->bzs', W1, W2)
        W3 = jnp.tril(W3)
        t = jnp.einsum('bzs,bsm->bzm', W3, n)
        t = _ln(_gelu(t), ln_g, ln_b)
        x1 = x + t
        out = x + _mlp(_ln(x1, ln_g, ln_b), fm_w1, fm_b1, fm_w2, fm_b2)
        return out

    def _L0_ffn_ref(hidden_states, rms_w, gate_w, w13, w2, sw_gate, sw_up, sw_down):
        import jax, jax.numpy as jnp
        import numpy as np
        H = 256
        I = 128
        E = 64
        K = 2
        EPS = 1e-06
        CAP = 256

        def _rmsnorm(x, w, eps=EPS):
            v = jnp.mean(x.astype(jnp.float32) ** 2, axis=-1, keepdims=True)
            return (x.astype(jnp.float32) * jax.lax.rsqrt(v + eps)).astype(x.dtype) * w
        B, S, Hh = hidden_states.shape
        residual = hidden_states
        x = _rmsnorm(hidden_states, rms_w).reshape(-1, Hh)
        T = x.shape[0]
        logits = x.astype(jnp.float32) @ gate_w.astype(jnp.float32).T
        probs = jax.nn.softmax(logits, axis=-1)
        topk_w, topk_ids = jax.lax.top_k(probs, K)
        topk_w = (topk_w / jnp.sum(topk_w, axis=-1, keepdims=True)).astype(x.dtype)
        flat_e = topk_ids.reshape(-1)
        order = jnp.argsort(flat_e)
        se = flat_e[order]
        tok = order // K
        counts = jax.ops.segment_sum(jnp.ones_like(se, jnp.int32), se, num_segments=E)
        starts = jnp.cumsum(counts) - counts
        pos = jnp.arange(se.shape[0]) - starts[se]
        pos_c = jnp.minimum(pos, CAP)
        buf = jnp.zeros((E, CAP + 1, Hh), x.dtype).at[se, pos_c].set(x[tok])
        xb = buf[:, :CAP]
        gu = jnp.einsum('ech,ehf->ecf', xb, w13)
        g, u = jnp.split(gu, 2, axis=-1)
        hact = jax.nn.silu(g) * u
        yb = jnp.einsum('eci,eih->ech', hact, w2)
        yb = jnp.concatenate([yb, jnp.zeros((E, 1, Hh), yb.dtype)], axis=1)
        y_slot = yb[se, pos_c]
        w_slot = topk_w.reshape(-1)[order]
        moe_out = jnp.zeros((T, Hh), x.dtype).at[tok].add(w_slot[:, None] * y_slot)
        shared = jax.nn.silu(x @ sw_gate) * (x @ sw_up) @ sw_down
        out = (moe_out + shared).reshape(B, S, Hh) + residual
        return out
    x = L0_attn_x
    x = x + 0.5 * _L0_ffn_ref(_layernorm(x, axis=-1), L0_ffn_rms_w, L0_ffn_gate_w, L0_ffn_w13, L0_ffn_w2, L0_ffn_sw_gate, L0_ffn_sw_up, L0_ffn_sw_down)
    x = x + _L0_attn_ref(_layernorm(x, axis=-1), L0_attn_ln_g, L0_attn_ln_b, L0_attn_h1_w1, L0_attn_h1_b1, L0_attn_h1_w2, L0_attn_h1_b2, L0_attn_h2_w1, L0_attn_h2_b1, L0_attn_h2_w2, L0_attn_h2_b2, L0_attn_fm_w1, L0_attn_fm_b1, L0_attn_fm_w2, L0_attn_fm_b2)
    x = x + 0.5 * _L0_ffn_ref(_layernorm(x, axis=-1), L0_ffn_rms_w, L0_ffn_gate_w, L0_ffn_w13, L0_ffn_w2, L0_ffn_sw_gate, L0_ffn_sw_up, L0_ffn_sw_down)
    return x

_drawn_inputs = setup_inputs


def setup_inputs(seed=0):
    import zlib

    import numpy as np

    out = dict(_drawn_inputs(seed))
    spreads = {'L0_attn_ln_g': (1.0, 0.2),
     'L0_attn_ln_b': (0.0, 0.1),
     'L0_attn_h1_b1': (0.0, 0.542),
     'L0_attn_h1_b2': (0.0, 0.348),
     'L0_attn_h2_b1': (0.0, 0.504),
     'L0_attn_h2_b2': (0.0, 0.296),
     'L0_attn_fm_b1': (0.0, 0.408),
     'L0_attn_fm_b2': (0.0, 0.1),
     'L0_ffn_rms_w': (1.0, 0.2)}
    factors = {}
    for name, (base, spread) in spreads.items():
        noise = np.random.default_rng([zlib.crc32(name.encode()), seed]).standard_normal(out[name].shape)
        drawn = base * np.exp(spread * noise) if base else spread * noise
        out[name] = jnp.asarray(drawn.astype(out[name].dtype))
    for name, factor in factors.items():
        out[name] = (out[name] * factor).astype(out[name].dtype)
    return out
```

```python
from contextlib import ExitStack

import concourse.bass as bass
import numpy as np
from concourse import mybir

fp32 = mybir.dt.float32
bf16 = mybir.dt.bfloat16
u32 = mybir.dt.uint32
ALU = mybir.AluOpType
ACT = mybir.ActivationFunctionType
AX = mybir.AxisListType
ds = bass.ds

P = 128
D = 256
KD = D // P
SEQS, SEQ = 8, 1024
TOKENS = SEQS * SEQ
TILES = TOKENS // P
GT = 4
GROUPS = TILES // GT
GW = GT * P
EXPERTS, INNER, CAP = 64, 128, 256
CH = CAP // P
SLOTS = EXPERTS * CAP
LN_EPS, RMS_EPS = 1e-5, 1e-6


class Count:

    def __init__(self, eng, sem, passed):
        self.eng, self.sem, self.passed = eng, sem, passed
        self.total, self.n, self.first = 0, 0, 0

    def enter(self, i, per):
        self.first, self.n, self.per = self.total + i * per, 0, per

    def leave(self, times):
        assert self.n == self.per, (self.n, self.per)
        self.total, self.n, self.first = self.total + times * self.per, 0, self.total + times * self.per

    def tick(self, ins):
        self.n += 1
        ins.then_inc(self.sem, 1)
        return ins

    def settle(self):
        self.eng.wait_ge(self.sem, self.first + self.n)

    def settle_alone(self):
        hold(self.eng, self.sem, self.first + self.n, self.passed)


def hold(eng, sem, value, passed):
    eng.wait_ge(sem, value)
    eng.sem_inc(passed, 1)


def rows(ap, g, tiles=GT):
    v = ap.rearrange("(g t p) n -> g p t n", t=tiles, p=P)
    return v[ds(g, 1), :, :, :].rearrange("a p t n -> p (a t) n")


class Kit:

    def __init__(self, nc, ctx, outer, tag):
        self.nc, self.ctx, self.outer, self.tag = nc, ctx, outer, tag

    def sb(self, name, shape, dt=fp32):
        return self.ctx.enter_context(self.nc.sbuf_tensor(f"{self.tag}_{name}", shape, dt))

    def ps(self, name, shape, dt=fp32):
        return self.ctx.enter_context(self.nc.psum_tensor(f"{self.tag}_{name}", shape, dt))

    def sem(self, name):
        return self.outer.enter_context(self.nc.semaphore(f"{self.tag}_{name}"))


def dispatch(nc, outer, tag, consts, routing, x, w, xn_d, base_d):
    with ExitStack() as ctx:
        kit = Kit(nc, ctx, outer, tag)
        sb, ps, sem = kit.sb, kit.ps, kit.sem
        gate = sb("gate", [P, KD, EXPERTS])
        sw_gate, sw_up = sb("sw_gate", [P, KD, INNER]), sb("sw_up", [P, KD, INNER])
        sw_down = sb("sw_down", [P, D])
        gate_rows = sb("gate_rows", [EXPERTS, D])
        rms_w = sb("rms_w", [P, GT, D])
        x_in = [sb(f"x_in{s}", [P, GT, D]) for s in range(2)]
        normed = [sb(f"normed{s}", [P, GT, D]) for s in range(2)]
        xn = [sb(f"xn{s}", [P, GT, D]) for s in range(2)]
        base = [sb(f"base{s}", [P, GT, D]) for s in range(2)]
        xn_t = [sb(f"xn_t{s}", [P, KD, GW]) for s in range(2)]
        silu = [sb(f"silu{s}", [P, GW]) for s in range(2)]
        hidden = [sb(f"hidden{s}", [P, GW]) for s in range(2)]
        stats = [sb(f"stats{s}", [P, GT, 6]) for s in range(2)]
        mean_var = [sb(f"mean_var{s}", [P, GT, 2]) for s in range(2)]
        small = [[sb(f"small{s}_{k}", [P, GT]) for k in range(10)] for s in range(2)]
        logits = [sb(f"logits{s}", [P, GT, EXPERTS]) for s in range(2)]
        top8 = [sb(f"top8_{s}", [P, GT, 8]) for s in range(2)]
        top8_at = [sb(f"top8_at{s}", [P, GT, 8], u32) for s in range(2)]
        chosen = [[sb(f"chosen{s}_{k}", [P, GT, EXPERTS], bf16) for k in range(2)] for s in range(2)]
        either = [sb(f"either{s}", [P, GT, EXPERTS], bf16) for s in range(2)]
        before = [sb(f"before{s}", [P, GT, EXPERTS], bf16) for s in range(2)]
        carry = sb("carry", [P, EXPERTS], bf16)
        place_in = [[sb(f"place_in{s}_{k}", [P, GT, EXPERTS]) for k in range(2)] for s in range(2)]
        at_place = [[sb(f"at_place{s}_{k}", [P, GT, CAP], bf16) for k in range(2)] for s in range(2)]
        token_of = [[sb(f"token_of{s}_{k}", [P, GT, 2, EXPERTS], bf16) for k in range(2)] for s in range(2)]
        expert_all = [sb(f"expert_all{k}", [P, TILES]) for k in range(2)]
        place_all = [sb(f"place_all{k}", [P, TILES]) for k in range(2)]
        gap_all = sb("gap_all", [P, TILES])
        late = sb("late", [P, TILES])
        slot_f = sb("slot_f", [P, 2, TILES])
        list_parts = sb("list_parts", [P, CH, 2, EXPERTS])
        list_f = sb("list_f", [P, CH, EXPERTS])
        ps_t = [ps(f"ps_t{k}", [P, GW]) for k in range(KD)]
        ps_route = ps("ps_route", [P, 2, GT, EXPERTS])
        ps_gate, ps_up = ps("ps_gate", [P, GW]), ps("ps_up", [P, GW])
        ps_down = [ps(f"ps_down{k}", [P, 2, D]) for k in range(2)]
        ps_list = ps("ps_list", [P, CH, 2, EXPERTS])

        loaded_w, gate_turned, gate_ready = sem("loaded_w"), sem("gate_turned"), sem("gate_ready")
        x_loaded = [sem(f"x_loaded{s}") for s in range(2)]
        x_used = sem("x_used")
        stats_ready, scales_ready, normed_ready = sem("stats_ready"), sem("scales_ready"), sem("normed_ready")
        xn_ready, xn_stored = sem("xn_ready"), [sem(f"xn_stored{s}") for s in range(2)]
        turned, xn_t_ready = sem("turned"), sem("xn_t_ready")
        logits_ready = sem("logits_ready")
        gate_up_ready, silu_ready, hidden_ready = sem("gate_up_ready"), sem("silu_ready"), sem("hidden_ready")
        chosen_ready, counts_ready = sem("chosen_ready"), sem("counts_ready")
        places_ready = sem("places_ready")
        at_place_ready, lists_added = sem("at_place_ready"), sem("lists_added")
        down_ready, base_ready = sem("down_ready"), sem("base_ready")
        base_stored = [sem(f"base_stored{s}") for s in range(2)]
        exp_ready, gap_ready = sem("exp_ready"), sem("gap_ready")
        dve_done, pool_done, passed = sem("dve_done"), sem("pool_done"), sem("passed")
        iota_e, iota_c = consts["iota_e"], consts["iota_c"]

        block = ctx.enter_context(nc.Block())

        @block.sync
        def _(sp):
            sp.dma_start(gate_rows[:, :], w["gate_w"]).then_inc(loaded_w, 16)
            sp.dma_start(sw_gate[:, :, :], w["sw_gate"].rearrange("(k p) n -> p k n", p=P)).then_inc(loaded_w, 16)
            sp.dma_start(sw_up[:, :, :], w["sw_up"].rearrange("(k p) n -> p k n", p=P)).then_inc(loaded_w, 16)
            sp.dma_start(sw_down[:, :], w["sw_down"]).then_inc(loaded_w, 16)
            for t in range(GT):
                sp.dma_start(rms_w[:, t, :], w["rms_w"].partition_broadcast(P)).then_inc(loaded_w, 16)
            for g in range(2):
                sp.dma_start(x_in[g][:, :, :], rows(x, g)).then_inc(x_loaded[g], 16)
            with sp.Fori(0, GROUPS // 2) as i:
                for s in range(2):
                    g = 2 * i + s
                    sp.wait_ge(xn_ready, g + 1)
                    sp.dma_start(rows(xn_d, g), xn[s][:, :, :]).then_inc(xn_stored[s], 16)
                    sp.wait_ge(x_used, g + 1)
                    sp.dma_start(x_in[s][:, :, :], rows(x, (g + 2) % GROUPS)).then_inc(x_loaded[s], 16)
                    sp.wait_ge(base_ready, g + 1)
                    sp.dma_start(rows(base_d, g), base[s][:, :, :]).then_inc(base_stored[s], 16)
            for s in range(2):
                sp.wait_ge(x_loaded[s], 16 * (GROUPS // 2 + 1))
                sp.wait_ge(xn_stored[s], 16 * (GROUPS // 2 + 1))
                sp.wait_ge(base_stored[s], 16 * (GROUPS // 2 + 1))

        @block.gpsimd
        def _(pool):
            done = Count(pool, pool_done, passed)
            for s in range(2):
                pool.sem_inc(xn_stored[s], 16)
            pool.memset(carry[:, :], 0.0).then_inc(pool_done, 1)
            done.total = 1

            def scales(i, s):
                g = 2 * i + s
                var_eps, r1, ms, ms_eps, r2, a, mn, b, c, d = small[s]
                mean, var = mean_var[s][:, :, 0], mean_var[s][:, :, 1]
                hold(pool, stats_ready, g + 1, passed)
                done.tick(pool.tensor_scalar(var_eps[:, :], var, LN_EPS, None, ALU.add))
                done.settle()
                done.tick(pool.tensor_tensor(r1[:, :], var_eps[:, :], consts["minus_half"][:, 0:GT], ALU.pow))
                done.settle()
                done.tick(pool.tensor_tensor(ms[:, :], var, r1[:, :], ALU.mult))
                done.tick(pool.tensor_tensor(mn[:, :], mean, r1[:, :], ALU.mult))
                done.settle()
                done.tick(pool.tensor_tensor(ms[:, :], ms[:, :], r1[:, :], ALU.mult))
                done.settle_alone()
                done.tick(pool.tensor_scalar(c[:, :], r1[:, :], 0.5, 1.0, ALU.mult, ALU.add))
                done.tick(pool.tensor_scalar(d[:, :], mn[:, :], -0.5, None, ALU.mult))
                done.tick(pool.tensor_scalar(ms_eps[:, :], ms[:, :], RMS_EPS, None, ALU.add))
                done.settle()
                done.tick(pool.tensor_tensor(r2[:, :], ms_eps[:, :], consts["minus_half"][:, 0:GT], ALU.pow))
                done.settle()
                done.tick(pool.tensor_tensor(a[:, :], r1[:, :], r2[:, :], ALU.mult))
                done.tick(pool.tensor_tensor(b[:, :], mn[:, :], r2[:, :], ALU.mult))
                done.settle_alone()
                done.tick(pool.tensor_scalar(b[:, :], b[:, :], -1.0, None, ALU.mult))
                done.settle()
                pool.sem_inc(scales_ready, 1)

            pool.sem_inc(counts_ready, 2)
            with pool.Fori(0, GROUPS // 2) as i:
                done.enter(i, 2 * 17)
                for s in range(2):
                    g = 2 * i + s
                    scales(i, s)
                    pool.wait_ge(normed_ready, g + 1)
                    pool.wait_ge(xn_stored[s], 16 * (i + 1))
                    pool.wait_ge(turned, g + 1)
                    pool.tensor_tensor(xn[s][:, :, :], normed[s][:, :, :], rms_w[:, :, :], ALU.mult).then_inc(xn_ready, 1)
                    pool.wait_ge(chosen_ready, g + 1)
                    for t in range(GT):
                        if t == 0:
                            pool.wait_ge(places_ready, g + 1)
                            done.settle_alone()
                            done.tick(pool.tensor_copy(before[s][:, 0, :], carry[:, :]))
                        else:
                            done.settle()
                            done.tick(pool.tensor_tensor(before[s][:, t, :], before[s][:, t - 1, :], either[s][:, t - 1, :], ALU.add))
                    done.settle()
                    done.tick(pool.tensor_tensor(carry[:, :], before[s][:, GT - 1, :], either[s][:, GT - 1, :], ALU.add))
                    done.settle()
                    pool.sem_inc(counts_ready, 1)
                done.leave(GROUPS // 2)

        @block.scalar
        def _(act):
            for s in range(2):
                act.sem_inc(base_stored[s], 16)
            act.wait_ge(gate_turned, 1)
            act.activation(gate[:, :, :], ps_t[0][:, 0:KD * EXPERTS].rearrange("p (k e) -> p k e", k=KD), ACT.Copy).then_inc(gate_ready, 1)
            with act.Fori(0, GROUPS // 2) as i:
                for s in range(2):
                    g = 2 * i + s
                    a, b, c, d = small[s][5], small[s][7], small[s][8], small[s][9]
                    act.wait_ge(scales_ready, g + 1)
                    act.wait_ge(base_stored[s], 16 * (i + 1))
                    for t in range(GT):
                        last = act.activation(normed[s][:, t, :], x_in[s][:, t, :], ACT.Identity, bias=b[:, t:t + 1], scale=a[:, t:t + 1])
                    last.then_inc(normed_ready, 1)
                    for t in range(GT):
                        last = act.activation(base[s][:, t, :], x_in[s][:, t, :], ACT.Identity, bias=d[:, t:t + 1], scale=c[:, t:t + 1])
                    last.then_inc(x_used, 1)
                    act.wait_ge(turned, g + 3)
                    for k in range(KD):
                        last = act.activation(xn_t[s][:, k, :], ps_t[k][:, :], ACT.Copy)
                    last.then_inc(xn_t_ready, 1)
                    act.wait_ge(gate_up_ready, g + 1)
                    act.activation(silu[s][:, :], ps_gate[:, :], ACT.Silu).then_inc(silu_ready, 1)
            act.wait_ge(gap_ready, 1)
            act.activation(gap_all[:, :], gap_all[:, :], ACT.Exp).then_inc(exp_ready, 1)

        @block.vector
        def _(dve):
            done = Count(dve, dve_done, passed)

            def statistics(i, s):
                dve.wait_ge(x_loaded[s], 16 * (i + 1))
                for t in range(GT):
                    done.tick(dve.bn_stats(stats[s][:, t, :], x_in[s][:, t, :]))
                done.settle_alone()
                for t in range(GT):
                    done.tick(dve.bn_aggr(mean_var[s][:, t, :], stats[s][:, t, :]))
                done.settle()
                dve.sem_inc(stats_ready, 1)

            def choose(i, s):
                g = 2 * i + s
                dve.wait_ge(logits_ready, g + 1)
                done.tick(dve.tensor_copy(logits[s][:, :, :], ps_route[:, 0, :, :]))
                done.settle_alone()
                for t in range(GT):
                    done.tick(dve.max(top8[s][:, t, :], logits[s][:, t, :]))
                done.settle_alone()
                for t in range(GT):
                    done.tick(dve.max_index(top8_at[s][:, t, :], top8[s][:, t, :], logits[s][:, t, :]))
                done.tick(dve.tensor_tensor(gap_all[:, ds(g * GT, GT)], top8[s][:, :, 1], top8[s][:, :, 0], ALU.subtract))
                done.settle_alone()
                for k in range(2):
                    done.tick(dve.tensor_copy(expert_all[k][:, ds(g * GT, GT)], top8_at[s][:, :, k]))
                done.settle()
                for k in range(2):
                    done.tick(dve.tensor_tensor(
                        chosen[s][k][:, :, :], iota_e[:, :].unsqueeze(1).broadcast_to([P, GT, EXPERTS]),
                        expert_all[k][:, ds(g * GT, GT)].unsqueeze(2).broadcast_to([P, GT, EXPERTS]), ALU.is_equal))
                done.settle()
                dve.wait_ge(counts_ready, g + 1)
                done.tick(dve.tensor_tensor(either[s][:, :, :], chosen[s][0][:, :, :], chosen[s][1][:, :, :], ALU.add))
                done.settle()
                dve.sem_inc(chosen_ready, 1)
                dve.wait_ge(lists_added, g + 1)
                for k in range(2):
                    done.tick(dve.tensor_scalar(token_of[s][k][:, :, 0, :], chosen[s][k][:, :, :], consts["partition"][:, 0:1], None, ALU.mult))
                    done.tick(dve.tensor_tensor(
                        token_of[s][k][:, :, 1, :], chosen[s][k][:, :, :],
                        consts["tile"][:, ds(g * GT, GT)].unsqueeze(2).broadcast_to([P, GT, EXPERTS]), ALU.mult))

            def shared_hidden(i, s):
                g = 2 * i + s
                dve.wait_ge(silu_ready, g + 1)
                done.tick(dve.tensor_tensor(hidden[s][:, :], silu[s][:, :], ps_up[:, :], ALU.mult))
                done.settle()
                dve.sem_inc(hidden_ready, 1)

            def places(i, s):
                g = 2 * i + s
                dve.wait_ge(places_ready, g + 3)
                for k in range(2):
                    done.tick(dve.tensor_tensor(place_in[s][k][:, :, :], chosen[s][k][:, :, :], ps_route[:, 1, :, :], ALU.mult))
                done.settle_alone()
                for k in range(2):
                    done.tick(dve.tensor_reduce(place_all[k][:, ds(g * GT, GT)], place_in[s][k][:, :, :], AX.X, ALU.add))
                done.settle()
                for k in range(2):
                    for t in range(GT):
                        done.tick(dve.tensor_scalar(at_place[s][k][:, t, :], iota_c[:, :], place_all[k][:, ds(g * GT + t, 1)], None, ALU.is_equal))
                done.settle()
                dve.sem_inc(at_place_ready, 1)

            def add_shared(i, s):
                g = 2 * i + s
                dve.wait_ge(down_ready, g + 1)
                for k in range(2):
                    done.tick(dve.scalar_tensor_tensor(base[s][:, 2 * k:2 * k + 2, :], ps_down[k][:, :, :], 0.5, base[s][:, 2 * k:2 * k + 2, :], ALU.mult, ALU.add))
                done.settle()
                dve.sem_inc(base_ready, 1)

            done.enter(0, 8)
            statistics(0, 0)
            done.leave(1)
            with dve.Fori(0, GROUPS // 2) as i:
                done.enter(i, 84)
                for s in range(2):
                    if s == 0:
                        statistics(i, 1)
                    else:
                        statistics(i + 1, 0)
                    choose(i, s)
                    shared_hidden(i, s)
                    places(i, s)
                    add_shared(i, s)
                done.leave(GROUPS // 2)
            dve.sem_inc(gap_ready, 1)
            dve.wait_ge(lists_added, GROUPS + 3)
            last = Count(dve, dve_done, passed)
            last.total = last.first = done.total
            last.tick(dve.tensor_copy(list_parts[:, :, :, :], ps_list[:, :, :, :]))
            last.settle()
            last.tick(dve.scalar_tensor_tensor(list_f[:, :, :], list_parts[:, :, 1, :], float(P), list_parts[:, :, 0, :], ALU.mult, ALU.add))
            last.settle()
            last.tick(dve.tensor_copy(routing["lists"][:, :, :], list_f[:, :, :].rearrange("p c e -> p e c")))
            for k in range(2):
                last.tick(dve.tensor_scalar(late[:, :], place_all[k][:, :], float(CAP), float(2 * SLOTS), ALU.is_ge, ALU.mult))
                last.tick(dve.scalar_tensor_tensor(slot_f[:, k, :], expert_all[k][:, :], float(CAP), place_all[k][:, :], ALU.mult, ALU.add))
                last.settle()
                last.tick(dve.tensor_tensor(slot_f[:, k, :], slot_f[:, k, :], late[:, :], ALU.add))
                last.settle()
                last.tick(dve.tensor_scalar(slot_f[:, k, :], slot_f[:, k, :], float(SLOTS), None, ALU.min))
                last.settle()
                last.tick(dve.tensor_copy(routing["slots"][:, :, k], slot_f[:, k, :]))
            dve.wait_ge(exp_ready, 1)
            last.tick(dve.tensor_scalar(late[:, :], gap_all[:, :], 1.0, None, ALU.add))
            last.settle()
            last.tick(dve.reciprocal(late[:, :], late[:, :]))
            last.settle()
            last.tick(dve.tensor_scalar(routing["halves"][:, :, 0], late[:, :], 0.5, None, ALU.mult))
            last.settle()
            last.tick(dve.tensor_tensor(routing["halves"][:, :, 1], routing["halves"][:, :, 0], gap_all[:, :], ALU.mult))
            last.settle()

        @block.tensor
        def _(pe):
            pe.sem_inc(turned, 2)
            pe.sem_inc(places_ready, 2)
            pe.sem_inc(lists_added, 2)
            pe.wait_ge(loaded_w, 16 * (4 + GT))
            for k in range(KD):
                last = pe.transpose(ps_t[0][:, k * EXPERTS:(k + 1) * EXPERTS], gate_rows[:, k * P:(k + 1) * P], consts["eye"][0:EXPERTS, 0:EXPERTS])
            last.then_inc(gate_turned, 1)
            pe.wait_ge(gate_ready, 1)
            zeros = consts["zeros"]
            pe.matmul(ps_list[:, :, :, :].rearrange("p c a e -> p (c a e)"), zeros[:, 0:P], zeros[:, :], start=True, stop=False)

            def turn(g, s):
                pe.wait_ge(xn_ready, g + 1)
                for k in range(KD):
                    for t in range(GT):
                        last = pe.transpose(ps_t[k][:, t * P:(t + 1) * P], xn[s][:, t, k * P:(k + 1) * P], consts["eye"][:, :])
                last.then_inc(turned, 1)

            with pe.Fori(0, GROUPS // 2) as i:
                for s in range(2):
                    g = 2 * i + s
                    turn(g, s)
                    pe.wait_ge(xn_t_ready, g + 1)
                    for t in range(GT):
                        for k in range(KD):
                            last = pe.matmul(ps_route[:, 0, t, :], xn_t[s][:, k, t * P:(t + 1) * P], gate[:, k, :], start=(k == 0), stop=(k == KD - 1))
                    last.then_inc(logits_ready, 1)
                    for wt, out in ((sw_gate, ps_gate), (sw_up, ps_up)):
                        for k in range(KD):
                            last = pe.matmul(out[:, :], wt[:, k, :], xn_t[s][:, k, :], start=(k == 0), stop=(k == KD - 1))
                    last.then_inc(gate_up_ready, 1)
                    pe.wait_ge(counts_ready, g + 3)
                    for t in range(GT):
                        pe.matmul(ps_route[:, 1, t, :], consts["earlier"][:, :], either[s][:, t, :], start=True, stop=False)
                        last = pe.matmul(ps_route[:, 1, t, :], consts["ones"][:, :], before[s][:, t, :], start=False, stop=True)
                    last.then_inc(places_ready, 1)
                    pe.wait_ge(hidden_ready, g + 1)
                    for t in range(GT):
                        last = pe.matmul(ps_down[t // 2][:, t % 2, :], hidden[s][:, t * P:(t + 1) * P], sw_down[:, :], start=True, stop=True)
                    last.then_inc(down_ready, 1)
                    pe.wait_ge(at_place_ready, g + 1)
                    for k in range(2):
                        for t in range(GT):
                            for c in range(CH):
                                last = pe.matmul(
                                    ps_list[:, c, :, :], at_place[s][k][:, t, c * P:(c + 1) * P], token_of[s][k][:, t, :, :],
                                    start=False, stop=False, skip_group_check=True)
                    last.then_inc(lists_added, 1)
            pe.matmul(
                ps_list[:, :, :, :].rearrange("p c a e -> p (c a e)"), zeros[:, 0:P], zeros[:, :],
                start=False, stop=True).then_inc(lists_added, 1)


def experts(nc, outer, tag, consts, routing, w, xn_d, y_d):
    R = 4
    with ExitStack() as ctx:
        kit = Kit(nc, ctx, outer, tag)
        sb, ps, sem = kit.sb, kit.ps, kit.sem
        w13 = [sb(f"w13_{s}", [P, KD, 2 * INNER]) for s in range(R)]
        w2 = [sb(f"w2_{s}", [P, D]) for s in range(R)]
        who = [sb(f"who{s}", [P, CH], u32) for s in range(R)]
        xg = [sb(f"xg{s}", [P, CH, D]) for s in range(R)]
        xg_t = [sb(f"xg_t{s}", [P, KD, CAP]) for s in range(R)]
        silu = [sb(f"silu{s}", [P, CAP]) for s in range(R)]
        hidden = [sb(f"hidden{s}", [P, CAP]) for s in range(R)]
        y = [sb(f"y{s}", [P, CH, D]) for s in range(R)]
        ps_t = [ps(f"ps_t{s}", [P, KD, CAP]) for s in range(2)]
        ps_gu = [ps(f"ps_gu{s}", [P, 2, CAP]) for s in range(2)]
        ps_y = [ps(f"ps_y{s}", [P, CH, D]) for s in range(2)]

        w_loaded = [sem(f"w_loaded{s}") for s in range(R)]
        rows_loaded = [sem(f"rows_loaded{s}") for s in range(R)]
        y_stored = [sem(f"y_stored{s}") for s in range(R)]
        zero_filled, zero_stored = sem("zero_filled"), sem("zero_stored")
        zero_row = sb("zero_row", [1, D])
        turned, xg_t_ready, gate_up_ready = sem("turned"), sem("xg_t_ready"), sem("gate_up_ready")
        silu_ready, hidden_ready, y_ready, y_copied = sem("silu_ready"), sem("hidden_ready"), sem("y_ready"), sem("y_copied")
        pool_done, passed = sem("pool_done"), sem("passed")

        block = ctx.enter_context(nc.Block())

        @block.sync
        def _(sp):
            sp.wait_ge(zero_filled, 1)
            sp.dma_start(y_d[SLOTS:SLOTS + 1, :], zero_row[0:1, :]).then_inc(zero_stored, 16)

            def load(e, s):
                sp.dma_start(w13[s][:, :, :], w["w13"][ds(e, 1), :, :].rearrange("a (k p) f -> p (a k) f", p=P)).then_inc(w_loaded[s], 16)
                sp.dma_start(w2[s][:, :], w["w2"][ds(e, 1), :, :].rearrange("a p h -> p (a h)")).then_inc(w_loaded[s], 16)

            def store(e, s):
                sp.wait_ge(y_copied, e + 3)
                out = y_d[0:SLOTS, :].rearrange("(e c p) h -> e p c h", p=P, c=CH)
                sp.dma_start(out[ds(e, 1), :, :, :].rearrange("a p c h -> p (a c) h"), y[s][:, :, :]).then_inc(y_stored[s], 16)

            for s in range(R):
                load(s, s)
            with sp.Fori(0, EXPERTS // R - 1) as i:
                for s in range(R):
                    e = R * i + s
                    store(e, s)
                    load(e + R, s)
            for s in range(R):
                store(EXPERTS - R + s, s)
            for s in range(R):
                sp.wait_ge(y_stored[s], 16 * (EXPERTS // R + 1))
            sp.wait_ge(zero_stored, 16)

        @block.gpsimd
        def _(pool):
            with pool.Fori(0, EXPERTS // R) as i:
                for s in range(R):
                    e = R * i + s
                    hold(pool, turned, e + 1, passed)
                    pool.tensor_copy(who[s][:, :], routing["lists"][:, ds(e, 1), :].rearrange("p a c -> p (a c)")).then_inc(pool_done, 1)
                    hold(pool, pool_done, e + 1, passed)
                    for c in range(CH):
                        pool.indirect_dma_start(
                            out=xg[s][:, c, :], out_offset=None, in_=xn_d,
                            in_offset=bass.IndirectOffsetOnAxis(ap=who[s][:, c:c + 1], axis=0),
                        ).then_inc(rows_loaded[s], 16)

        @block.scalar
        def _(act):
            with act.Fori(0, EXPERTS // R) as i:
                for s in range(R):
                    e = R * i + s
                    act.wait_ge(turned, e + 1 + R)
                    act.activation(xg_t[s][:, :, :], ps_t[s % 2][:, :, :], ACT.Copy).then_inc(xg_t_ready, 1)
                    act.wait_ge(gate_up_ready, e + 1)
                    act.activation(silu[s][:, :], ps_gu[s % 2][:, 0, :], ACT.Silu).then_inc(silu_ready, 1)

        @block.vector
        def _(dve):
            dve.memset(zero_row[:, :], 0.0).then_inc(zero_filled, 1)
            for s in range(R):
                dve.sem_inc(y_stored[s], 16)
            with dve.Fori(0, EXPERTS // R) as i:
                for s in range(R):
                    e = R * i + s
                    dve.wait_ge(silu_ready, e + 1)
                    dve.tensor_tensor(hidden[s][:, :], silu[s][:, :], ps_gu[s % 2][:, 1, :], ALU.mult).then_inc(hidden_ready, 1)
                    dve.wait_ge(y_ready, e + 1)
                    dve.wait_ge(y_stored[s], 16 * (i + 1))
                    dve.tensor_copy(y[s][:, :, :], ps_y[s % 2][:, :, :]).then_inc(y_copied, 1)

        @block.tensor
        def _(pe):
            pe.sem_inc(turned, R)
            pe.sem_inc(y_copied, 2)

            def turn(e, i, s):
                pe.wait_ge(rows_loaded[s], 2 * 16 * (i + 1))
                for k in range(KD):
                    for c in range(CH):
                        last = pe.transpose(ps_t[s % 2][:, k, c * P:(c + 1) * P], xg[s][:, c, k * P:(k + 1) * P], consts["eye"][:, :])
                last.then_inc(turned, 1)

            def gate_up(e, i, s):
                pe.wait_ge(xg_t_ready, e + 1)
                pe.wait_ge(w_loaded[s], 2 * 16 * (i + 1))
                for half in range(2):
                    for k in range(KD):
                        last = pe.matmul(ps_gu[s % 2][:, half, :], w13[s][:, k, half * INNER:(half + 1) * INNER], xg_t[s][:, k, :], start=(k == 0), stop=(k == KD - 1))
                last.then_inc(gate_up_ready, 1)

            def down(e, s):
                pe.wait_ge(hidden_ready, e + 1)
                for c in range(CH):
                    last = pe.matmul(ps_y[s % 2][:, c, :], hidden[s][:, c * P:(c + 1) * P], w2[s][:, :], start=True, stop=True)
                last.then_inc(y_ready, 1)

            turn(0, 0, 0)
            gate_up(0, 0, 0)
            with pe.Fori(0, EXPERTS // R - 1) as i:
                for s in range(R):
                    e = R * i + s
                    nxt, j = (s + 1) % R, i + (s + 1) // R
                    turn(e + 1, j, nxt)
                    pe.wait_ge(y_copied, e + 1)
                    down(e, s)
                    gate_up(e + 1, j, nxt)
            for s in range(R):
                e, i = EXPERTS - R + s, EXPERTS // R - 1
                if s + 1 < R:
                    turn(e + 1, i, s + 1)
                pe.wait_ge(y_copied, e + 1)
                down(e, s)
                if s + 1 < R:
                    gate_up(e + 1, i, s + 1)


def combine(nc, outer, tag, consts, routing, base_d, y_d, out):
    with ExitStack() as ctx:
        kit = Kit(nc, ctx, outer, tag)
        sb, sem = kit.sb, kit.sem
        R = 4
        acc = [sb(f"acc{s}", [P, GT, D]) for s in range(R)]
        ye = [sb(f"ye{s}", [P, GT, 2, D]) for s in range(R)]
        where = [sb(f"where{s}", [P, GT, 2], u32) for s in range(R)]
        half = [sb(f"half{s}", [P, GT, 2]) for s in range(R)]
        base_loaded, rows_loaded = [sem(f"base_loaded{s}") for s in range(R)], [sem(f"rows_loaded{s}") for s in range(R)]
        stored = [sem(f"stored{s}") for s in range(R)]
        added, added_rows, pool_done, dve_done, passed = sem("added"), sem("added_rows"), sem("pool_done"), sem("dve_done"), sem("passed")
        block = ctx.enter_context(nc.Block())

        @block.sync
        def _(sp):
            for s in range(R):
                sp.dma_start(acc[s][:, :, :], rows(base_d, s)).then_inc(base_loaded[s], 16)
            with sp.Fori(0, GROUPS // R - 1) as i:
                for s in range(R):
                    g = R * i + s
                    sp.wait_ge(added, g + 1)
                    sp.dma_start(rows(out, g), acc[s][:, :, :]).then_inc(stored[s], 16)
                    sp.wait_ge(stored[s], 16 * (i + 1))
                    sp.dma_start(acc[s][:, :, :], rows(base_d, g + R)).then_inc(base_loaded[s], 16)
            for s in range(R):
                sp.wait_ge(added, GROUPS - R + s + 1)
                sp.dma_start(rows(out, GROUPS - R + s), acc[s][:, :, :]).then_inc(stored[s], 16)
            for s in range(R):
                sp.wait_ge(stored[s], 16 * (GROUPS // R))

        @block.gpsimd
        def _(pool):
            pool.sem_inc(added_rows, R)
            with pool.Fori(0, GROUPS // R) as i:
                for s in range(R):
                    g = R * i + s
                    hold(pool, added_rows, g + 1, passed)
                    pool.tensor_copy(where[s][:, :, :], routing["slots"][:, ds(g * GT, GT), :]).then_inc(pool_done, 1)
                    hold(pool, pool_done, g + 1, passed)
                    for t in range(GT):
                        for k in range(2):
                            pool.indirect_dma_start(
                                out=ye[s][:, t, k, :], out_offset=None, in_=y_d,
                                in_offset=bass.IndirectOffsetOnAxis(ap=where[s][:, t, k:k + 1], axis=0),
                            ).then_inc(rows_loaded[s], 16)

        @block.vector
        def _(dve):
            done = Count(dve, dve_done, passed)
            with dve.Fori(0, GROUPS // R) as i:
                done.enter(i, R * (1 + 2 * GT))
                for s in range(R):
                    g = R * i + s
                    done.tick(dve.tensor_copy(half[s][:, :, :], routing["halves"][:, ds(g * GT, GT), :]))
                    done.settle()
                    dve.wait_ge(base_loaded[s], 16 * (i + 1))
                    dve.wait_ge(rows_loaded[s], 16 * 2 * GT * (i + 1))
                    for k in range(2):
                        for t in range(GT):
                            done.tick(dve.scalar_tensor_tensor(acc[s][:, t, :], ye[s][:, t, k, :], half[s][:, t, k:k + 1], acc[s][:, t, :], ALU.mult, ALU.add))
                        done.settle()
                    dve.sem_inc(added, 1)
                    dve.sem_inc(added_rows, 1)
                done.leave(GROUPS // R)


def attention(nc, outer, tag, consts, routing, w, base_d, y_d, x2_d):
    fr = mybir.dt.float32r
    FC = 1024 // P
    RING, GELUS, PARTS, LAG = 4, 2, 3, 2
    H1, H2, FM = range(3)
    CHUNKS = 6 * FC
    USES = CHUNKS + 3 * GT
    chunk0 = {(H1, 0): 0, (H2, 0): FC, (H1, 1): 2 * FC, (H2, 1): 3 * FC, (FM, 0): 4 * FC, (FM, 1): 5 * FC}
    use0 = {(H1, 0): 0, (H2, 0): FC, "scores0": 2 * FC, (H1, 1): 2 * FC + GT, (H2, 1): 3 * FC + GT,
            "scores1": 4 * FC + GT, (FM, 0): 4 * FC + 3 * GT, (FM, 1): 5 * FC + 3 * GT}
    group0 = {(H1, 0): 0, (H2, 0): 1, (H1, 1): 2, (H2, 1): 3, (FM, 0): 4, (FM, 1): 5}
    W_N1, W_T0, W_M0, W_T1, W_M1, W_N0_NEXT = range(6)
    R_N0, R_N1, R_M0, R_M1 = range(4)
    S_N0, S_N1, S_T0, S_M0, S_T1, S_M1 = range(6)
    with ExitStack() as ctx:
        kit = Kit(nc, ctx, outer, tag)
        sb, ps, sem = kit.sb, kit.ps, kit.sem
        w1 = [[sb(f"w1_{m}_{part}", [P, KD, FC * P], fr) for part in "hl"] for m in range(3)]
        w2 = [[sb(f"w2_{m}_{part}", [P, FC, D], fr) for part in "hl"] for m in range(3)]
        b1 = sb("b1", [P, 3, FC])
        b2 = sb("b2", [P, 2, KD])
        g_row, b_row, b2_row = sb("g_row", [P, D]), sb("b_row", [P, D]), sb("b2_row", [P, D])
        rows_t = [[sb(f"rows_t{h}_{part}", [P, KD, GW], fr) for part in "hl"] for h in range(2)]
        gelu = [sb(f"gelu{j}", [P, GW]) for j in range(GELUS)]
        hid = [[sb(f"hid{j}_{part}", [P, GW], fr) for part in "hl"] for j in range(PARTS)]
        proj_t = [sb(f"proj_t{m}", [P, KD, SEQ]) for m in range(2)]
        score_at = [GW * i for i in range(GT)] + [GT * GW + sum(GW - P * e for e in range(d)) for d in range(GT)]
        scores = sb("scores", [P, score_at[-1] + P])
        n_rows = sb("n_rows", [P, 2 * GT, D])
        x1, z = sb("x1", [P, 2 * GT, D]), sb("z", [P, 2 * GT, D])
        base_in = sb("base_in", [P, GT, D])
        ye = sb("ye", [P, GT, 2, D])
        where, half = sb("where", [P, GT, 2], u32), sb("half", [P, GT, 2])
        t_rows = sb("t_rows", [P, GT, D])
        stats, mean_var = sb("stats", [P, GT, 6]), sb("mean_var", [P, GT, 2])
        var_eps, r1, var_z, r2, rr = [sb(f"small{k}", [P, GT]) for k in range(5)]
        ring = [ps(f"ring{j}", [P, GW]) for j in range(RING)]
        acc = [ps(f"acc{j}", [P, GW]) for j in range(2)]
        work = [ps(f"work{j}", [P, GW]) for j in range(2)]

        w_loaded, w_split = [sem(f"w_loaded{j}") for j in range(2)], sem("w_split")
        b_loaded = sem("b_loaded")
        base_loaded, rows_loaded, rows_used, x_stored = sem("base_loaded"), sem("rows_loaded"), sem("rows_used"), sem("x_stored")
        ring_full, ring_free = sem("ring_full"), sem("ring_free")
        hid_ready, hid_used = sem("hid_ready"), sem("hid_used")
        acc_free = sem("acc_free")
        work_full, work_free = sem("work_full"), sem("work_free")
        hi_ready, turned_ready = sem("hi_ready"), sem("turned_ready")
        masked, rows_ready = sem("masked"), sem("rows_ready")
        stats_ready, scales_ready, sums_ready = sem("stats_ready"), sem("scales_ready"), sem("sums_ready")
        out_ready = sem("out_ready")
        dve_done, pool_done, passed = sem("dve_done"), sem("pool_done"), sem("passed")
        staging = [a[:, :, :].rearrange("p a b -> p (a b)") for a in (x1, z)]
        names = ("h1", "h2", "fm")

        def score_tile(i, lo, hi):
            start = score_at[i] - (i - GT) * P if i >= GT else score_at[i]
            return scores[:, start + lo:start + hi]

        block = ctx.enter_context(nc.Block())

        @block.sync
        def _(sp):
            for m, name in enumerate(names):
                if m > 0:
                    sp.wait_ge(w_split, 2 * m - 1)
                sp.dma_start(staging[0].rearrange("p (k f) -> p k f", k=KD), w[name + "_w1"].rearrange("(k p) f -> p k f", p=P)).then_inc(w_loaded[0], 16)
                if m > 0:
                    sp.wait_ge(w_split, 2 * m)
                sp.dma_start(staging[1].rearrange("p (c d) -> p c d", c=FC), w[name + "_w2"].rearrange("(c p) d -> p c d", p=P)).then_inc(w_loaded[1], 16)
                if m == 0:
                    sp.dma_start(base_in[:, :, :], rows(base_d, 0)).then_inc(base_loaded, 16)
                    for j, n2 in enumerate(names):
                        sp.dma_start(b1[:, j, :], w[n2 + "_b1"].rearrange("(c p) -> p c", p=P), allow_slow_non_contiguous=True).then_inc(b_loaded, 16)
                    for j, n2 in enumerate(names[:2]):
                        sp.dma_start(b2[:, j, :], w[n2 + "_b2"].rearrange("(k p) -> p k", p=P), allow_slow_non_contiguous=True).then_inc(b_loaded, 16)
                    for row, n2 in ((g_row, "ln_g"), (b_row, "ln_b"), (b2_row, "fm_b2")):
                        sp.dma_start(row[:, :], w[n2].partition_broadcast(P)).then_inc(b_loaded, 16)

            def load_base(g):
                sp.wait_ge(rows_used, g + 1)
                sp.dma_start(base_in[:, :, :], rows(base_d, g)).then_inc(base_loaded, 16)

            def store(b, h):
                sp.wait_ge(out_ready, 2 * b + h + 1)
                sp.dma_start(rows(x2_d, 2 * b + h), x1[:, GT * h:GT * (h + 1), :]).then_inc(x_stored, 16)

            load_base(1)
            with sp.Fori(0, SEQS - 1) as b:
                load_base(2 * b + 2)
                store(b, 0)
                load_base(2 * b + 3)
                store(b, 1)
            store(SEQS - 1, 0)
            store(SEQS - 1, 1)
            sp.wait_ge(x_stored, 16 * (2 * SEQS + 2))

        @block.gpsimd
        def _(pool):
            done = Count(pool, pool_done, passed)
            pool.sem_inc(rows_used, 1)
            pool.wait_ge(b_loaded, 16 * 8)

            def gather(b, h):
                g = 2 * b + h
                hold(pool, rows_used, g + 1, passed)
                done.settle_alone()
                done.tick(pool.tensor_copy(where[:, :, :], routing["slots"][:, ds(g * GT, GT), :]))
                done.settle_alone()
                for t in range(GT):
                    for k in range(2):
                        pool.indirect_dma_start(
                            out=ye[:, t, k, :], out_offset=None, in_=y_d,
                            in_offset=bass.IndirectOffsetOnAxis(ap=where[:, t, k:k + 1], axis=0),
                        ).then_inc(rows_loaded, 16)

            def scales(b, order, twice):
                hold(pool, stats_ready, 6 * b + order + 1, passed)
                var = mean_var[:, :, 1]
                done.tick(pool.tensor_scalar(var_eps[:, :], var, LN_EPS, None, ALU.add))
                done.settle()
                done.tick(pool.tensor_tensor(r1[:, :], var_eps[:, :], consts["minus_half"][:, 0:GT], ALU.pow))
                if twice:
                    done.settle()
                    done.tick(pool.tensor_tensor(var_z[:, :], var, r1[:, :], ALU.mult))
                    done.settle()
                    done.tick(pool.tensor_tensor(var_z[:, :], var_z[:, :], r1[:, :], ALU.mult))
                    done.settle_alone()
                    done.tick(pool.tensor_scalar(var_z[:, :], var_z[:, :], LN_EPS, None, ALU.add))
                    done.settle()
                    done.tick(pool.tensor_tensor(r2[:, :], var_z[:, :], consts["minus_half"][:, 0:GT], ALU.pow))
                    done.settle()
                    done.tick(pool.tensor_tensor(rr[:, :], r1[:, :], r2[:, :], ALU.mult))
                done.settle()
                pool.sem_inc(scales_ready, 1)

            def sums(b, h):
                xs, zs = x1[:, GT * h:GT * (h + 1), :], z[:, GT * h:GT * (h + 1), :]
                pool.wait_ge(rows_ready, 4 * b + h + 1)
                done.tick(pool.tensor_tensor(xs, xs, zs, ALU.add))
                done.settle()
                done.tick(pool.tensor_tensor(xs, xs, b2_row[:, :].unsqueeze(1).broadcast_to([P, GT, D]), ALU.add))
                done.tick(pool.tensor_tensor(zs, zs, b_row[:, :].unsqueeze(1).broadcast_to([P, GT, D]), ALU.add))
                done.settle()
                pool.sem_inc(sums_ready, 1)

            def mask(b, h):
                for d in range(GT):
                    i = GT * h + d
                    hold(pool, ring_free, USES * b + use0[f"scores{h}"] + i + RING + 1, passed)
                    tile = score_tile(i, d * P, (d + 1) * P)
                    pool.affine_select(out=tile, in_=tile, compare_op=ALU.is_ge, fill=0.0, base=0,
                                       pattern=[[1, P]], channel_multiplier=-1).then_inc(masked, 1)

            def sequence(b, more):
                scales(b, S_N1, True)
                if more:
                    gather(b + 1, 0)
                sums(b, 1)
                mask(b, 0)
                scales(b, S_T0, False)
                scales(b, S_M0, False)
                mask(b, 1)
                scales(b, S_T1, False)
                scales(b, S_M1, False)
                if more:
                    scales(b + 1, S_N0, True)
                    gather(b + 1, 1)
                    sums(b + 1, 0)

            done.enter(0, 12)
            gather(0, 0)
            scales(0, S_N0, True)
            gather(0, 1)
            sums(0, 0)
            done.leave(1)
            with pool.Fori(0, SEQS - 1) as b:
                done.enter(b, 2 * 7 + 4 * 2 + 2 * 3 + 2)
                sequence(b, True)
                done.leave(SEQS - 1)
            done.enter(0, 7 + 4 * 2 + 3)
            sequence(SEQS - 1, False)
            done.leave(1)

        @block.scalar
        def _(act):
            act.sem_inc(ring_free, RING)
            act.sem_inc(work_free, 1)
            act.wait_ge(b_loaded, 16 * 8)

            def mlp_chunk(b, m, h, c):
                n = CHUNKS * b + chunk0[m, h] + c
                j = (chunk0[m, h] + c)
                act.wait_ge(ring_full, USES * b + use0[m, h] + c + 1)
                act.wait_ge(hid_used, n + 1)
                act.wait_ge(hid_ready, n + 1)
                src = ring[(use0[m, h] + c) % RING][:, :]
                act.activation(hid[j % PARTS][0][:, :], src, ACT.Gelu, bias=b1[:, m, c:c + 1])
                act.activation(gelu[j % GELUS][:, :], src, ACT.Gelu, bias=b1[:, m, c:c + 1]).then_inc(ring_free, 1)

            def score_tiles(b, h):
                for i in range(GT * (h + 1)):
                    lo = max(i - GT * h, 0) * P
                    use = use0[f"scores{h}"] + i
                    act.wait_ge(ring_full, USES * b + use + 1)
                    act.activation(score_tile(i, lo, GW), ring[use % RING][:, lo:GW], ACT.Copy).then_inc(ring_free, 1)

            def turned_hi(b, v, h):
                act.wait_ge(work_full, 6 * b + v + 2)
                for k in range(KD):
                    last = act.activation(rows_t[h][0][:, k, :], work[k][:, :], ACT.Copy)
                last.then_inc(hi_ready, 1)

            def t_gelu(b, v, h):
                act.wait_ge(work_full, 6 * b + v + 2)
                for j in range(2):
                    last = act.activation(t_rows[:, 2 * j:2 * j + 2, :], work[j][:, :].rearrange("p (t d) -> p t d", t=2), ACT.Gelu)
                last.then_inc(work_free, 1)

            def sequence(b, more):
                for m in (H1, H2):
                    for c in range(FC):
                        mlp_chunk(b, m, 0, c)
                score_tiles(b, 0)
                turned_hi(b, W_N1, 1)
                t_gelu(b, W_T0, 0)
                for m in (H1, H2):
                    for c in range(FC):
                        mlp_chunk(b, m, 1, c)
                score_tiles(b, 1)
                turned_hi(b, W_M0, 0)
                t_gelu(b, W_T1, 1)
                for c in range(FC):
                    mlp_chunk(b, FM, 0, c)
                turned_hi(b, W_M1, 1)
                for c in range(FC):
                    if c == FC - 1 and more:
                        turned_hi(b, W_N0_NEXT, 0)
                    mlp_chunk(b, FM, 1, c)

            turned_hi(0, -1, 0)
            with act.Fori(0, SEQS - 1) as b:
                sequence(b, True)
            sequence(SEQS - 1, False)

        @block.vector
        def _(dve):
            done = Count(dve, dve_done, passed)
            dve.sem_inc(hid_ready, GELUS)
            dve.sem_inc(acc_free, 1)
            dve.sem_inc(x_stored, 2 * 16)
            split = 0
            for m in range(3):
                for j, parts in enumerate((w1[m], w2[m])):
                    hi, lo = [p[:, :, :].rearrange("p a b -> p (a b)") for p in parts]
                    dve.wait_ge(w_loaded[j], 16 * (m + 1))
                    done.tick(dve.tensor_copy(hi, staging[j]))
                    done.settle()
                    done.tick(dve.tensor_tensor(lo, staging[j], hi.bitcast(fp32), ALU.subtract))
                    done.settle()
                    dve.sem_inc(w_split, 1)
            done.total, done.n = done.n, 0
            dve.wait_ge(b_loaded, 16 * 8)

            def add_rows(b, h):
                g = 2 * b + h
                done.tick(dve.tensor_copy(half[:, :, :], routing["halves"][:, ds(g * GT, GT), :]))
                done.settle()
                dve.wait_ge(x_stored, 16 * (g + 1))
                dve.wait_ge(base_loaded, 16 * (g + 1))
                dve.wait_ge(rows_loaded, 16 * 2 * GT * (g + 1))
                for t in range(GT):
                    done.tick(dve.scalar_tensor_tensor(x1[:, GT * h + t, :], ye[:, t, 0, :], half[:, t, 0:1], base_in[:, t, :], ALU.mult, ALU.add))
                done.settle()
                for t in range(GT):
                    done.tick(dve.scalar_tensor_tensor(x1[:, GT * h + t, :], ye[:, t, 1, :], half[:, t, 1:2], x1[:, GT * h + t, :], ALU.mult, ALU.add))
                done.settle()
                dve.sem_inc(rows_used, 1)

            def statistics(src):
                for t in range(GT):
                    done.tick(dve.bn_stats(stats[:, t, :], src[:, t, :]))
                done.settle_alone()
                for t in range(GT):
                    done.tick(dve.bn_aggr(mean_var[:, t, :], stats[:, t, :]))
                done.settle()
                dve.sem_inc(stats_ready, 1)

            def centred(dst, src):
                for t in range(GT):
                    done.tick(dve.scalar_tensor_tensor(dst[:, t, :], src[:, t, :], mean_var[:, t, 0:1], g_row[:, :], ALU.subtract, ALU.mult))
                done.settle()

            def normalise(b, h):
                xs, zs, ns = [a[:, GT * h:GT * (h + 1), :] for a in (x1, z, n_rows)]
                dve.wait_ge(scales_ready, 6 * b + h + 1)
                for t in range(GT):
                    done.tick(dve.tensor_scalar(zs[:, t, :], xs[:, t, :], mean_var[:, t, 0:1], r1[:, t:t + 1], ALU.subtract, ALU.mult))
                centred(ns, xs)
                for t in range(GT):
                    done.tick(dve.scalar_tensor_tensor(ns[:, t, :], ns[:, t, :], rr[:, t:t + 1], b_row[:, :], ALU.mult, ALU.add))
                done.settle()
                dve.sem_inc(rows_ready, 1)

            def residual(b, h):
                dve.wait_ge(scales_ready, 6 * b + (S_T0, S_T1)[h] + 1)
                centred(t_rows, t_rows)
                dve.wait_ge(sums_ready, 2 * b + h + 1)
                for t in range(GT):
                    done.tick(dve.scalar_tensor_tensor(t_rows[:, t, :], t_rows[:, t, :], r1[:, t:t + 1], z[:, GT * h + t, :], ALU.mult, ALU.add))
                done.settle_alone()
                statistics(t_rows)

            def m_rows(b, h):
                dve.wait_ge(scales_ready, 6 * b + (S_M0, S_M1)[h] + 1)
                centred(t_rows, t_rows)
                for t in range(GT):
                    done.tick(dve.scalar_tensor_tensor(t_rows[:, t, :], t_rows[:, t, :], r1[:, t:t + 1], b_row[:, :], ALU.mult, ALU.add))
                done.settle()
                dve.sem_inc(rows_ready, 1)

            def rest(b, m, h, c):
                n = chunk0[m, h] + c
                dve.wait_ge(ring_free, USES * b + use0[m, h] + c + RING + 1)
                dve.tensor_tensor(hid[n % PARTS][1][:, :], gelu[n % GELUS][:, :], hid[n % PARTS][0][:, :].bitcast(fp32), ALU.subtract).then_inc(hid_ready, 1)

            def project(b, m, h):
                dve.wait_ge(hid_used, CHUNKS * b + chunk0[m, h] + FC + PARTS)
                for k in range(KD):
                    last = dve.tensor_scalar(proj_t[m][:, k, GW * h:GW * (h + 1)], acc[k][:, :], b2[:, m, k:k + 1], None, ALU.add)
                    done.tick(last)
                done.settle()
                dve.sem_inc(acc_free, 1)

            def turned_rest(b, order, h):
                dve.wait_ge(hi_ready, 4 * b + order + 1)
                for k in range(KD):
                    done.tick(dve.tensor_tensor(rows_t[h][1][:, k, :], work[k][:, :], rows_t[h][0][:, k, :].bitcast(fp32), ALU.subtract))
                done.settle()
                dve.sem_inc(work_free, 1)
                dve.sem_inc(turned_ready, 1)

            def add_out(b, h):
                dve.wait_ge(hid_used, CHUNKS * b + chunk0[FM, h] + FC + PARTS)
                for j in range(2):
                    xs = x1[:, GT * h + 2 * j:GT * h + 2 * j + 2, :]
                    done.tick(dve.tensor_tensor(xs, xs, acc[j][:, :].rearrange("p (t d) -> p t d", t=2), ALU.add))
                done.settle()
                dve.sem_inc(acc_free, 1)
                dve.sem_inc(out_ready, 1)

            def sequence(b, more):
                for c in range(FC):
                    rest(b, H1, 0, c)
                    if c == 3:
                        add_rows(b, 1)
                    if c == 5:
                        statistics(x1[:, GT:2 * GT, :])
                project(b, H1, 0)
                for c in range(FC):
                    rest(b, H2, 0, c)
                    if c == 1:
                        normalise(b, 1)
                project(b, H2, 0)
                turned_rest(b, R_N1, 1)
                for c in range(FC):
                    rest(b, H1, 1, c)
                    if c == 1:
                        dve.wait_ge(work_free, 6 * b + W_T0 + 3)
                        statistics(t_rows)
                    if c == 3:
                        residual(b, 0)
                    if c == 6:
                        m_rows(b, 0)
                project(b, H1, 1)
                for c in range(FC):
                    rest(b, H2, 1, c)
                project(b, H2, 1)
                turned_rest(b, R_M0, 0)
                for c in range(FC):
                    rest(b, FM, 0, c)
                    if c == 0:
                        dve.wait_ge(work_free, 6 * b + W_T1 + 3)
                        statistics(t_rows)
                    if c == 2:
                        residual(b, 1)
                    if c == 4:
                        m_rows(b, 1)
                add_out(b, 0)
                turned_rest(b, R_M1, 1)
                for c in range(FC):
                    if c == FC - 1 and more:
                        turned_rest(b + 1, R_N0, 0)
                    rest(b, FM, 1, c)
                    if more:
                        if c == 0:
                            add_rows(b + 1, 0)
                        if c == 2:
                            statistics(x1[:, 0:GT, :])
                        if c == 4:
                            normalise(b + 1, 0)
                add_out(b, 1)

            done.enter(0, 9 + 8 + 12 + 2)
            add_rows(0, 0)
            statistics(x1[:, 0:GT, :])
            normalise(0, 0)
            turned_rest(0, R_N0, 0)
            done.leave(1)
            with dve.Fori(0, SEQS - 1) as b:
                done.enter(b, 142)
                sequence(b, True)
                done.leave(SEQS - 1)
            done.enter(0, 111)
            sequence(SEQS - 1, False)
            done.leave(1)

        @block.tensor
        def _(pe):
            pe.sem_inc(hid_used, PARTS)
            pe.wait_ge(w_split, 6)
            TERMS = ((0, 0), (1, 0), (0, 1))

            def turn(b, order, v, src):
                pe.wait_ge(rows_ready, 4 * b + order + 1)
                pe.wait_ge(work_free, 6 * b + v + 2)
                for k in range(KD):
                    for t in range(GT):
                        last = pe.transpose(work[k][:, t * P:(t + 1) * P], src[:, t, k * P:(k + 1) * P], consts["eye"][:, :])
                last.then_inc(work_full, 1)

            def up(b, m, h, c):
                use = use0[m, h] + c
                pe.wait_ge(ring_free, USES * b + use + 1)
                n = 0
                for k in range(KD):
                    for wp, xp in TERMS:
                        last = pe.matmul(ring[use % RING][:, :], w1[m][wp][:, k, c * P:(c + 1) * P], rows_t[h][xp][:, k, :], start=(n == 0), stop=(n == 2 * len(TERMS) - 1))
                        n += 1
                last.then_inc(ring_full, 1)

            def down(b, m, h, c):
                j = (chunk0[m, h] + c) % PARTS
                if c == 0:
                    pe.wait_ge(acc_free, 6 * b + group0[m, h] + 1)
                pe.wait_ge(hid_ready, CHUNKS * b + chunk0[m, h] + c + GELUS + 1)
                if m == FM:
                    for t in range(GT):
                        for q, (wp, xp) in enumerate(TERMS):
                            last = pe.matmul(acc[t // 2][:, (t % 2) * D:(t % 2 + 1) * D], hid[j][xp][:, t * P:(t + 1) * P], w2[m][wp][:, c, :],
                                             start=(c == 0 and q == 0 and t % 2 == 0), stop=(c == FC - 1 and q == 2), skip_group_check=True)
                else:
                    for k in range(KD):
                        for q, (wp, xp) in enumerate(TERMS):
                            last = pe.matmul(acc[k][:, :], w2[m][wp][:, c, k * P:(k + 1) * P], hid[j][xp][:, :], start=(c == 0 and q == 0), stop=(c == FC - 1 and q == 2))
                last.then_inc(hid_used, 1)

            def mlp(b, m, h, more=False):
                for c in range(FC):
                    if c == FC - 1 and more:
                        turn(b + 1, R_N0, W_N0_NEXT - 6, n_rows[:, 0:GT, :])
                    if c == 0:
                        pe.wait_ge(turned_ready, 4 * b + {(H1, 0): R_N0, (H2, 0): R_N0, (H1, 1): R_N1, (H2, 1): R_N1, (FM, 0): R_M0, (FM, 1): R_M1}[m, h] + 1)
                    up(b, m, h, c)
                    if c >= LAG:
                        down(b, m, h, c - LAG)
                for c in range(FC - LAG, FC):
                    down(b, m, h, c)

            def score_tiles(b, h):
                for i in range(GT * (h + 1)):
                    lo = max(i - GT * h, 0) * P
                    use = use0[f"scores{h}"] + i
                    pe.wait_ge(ring_free, USES * b + use + 1)
                    if i % GT == 0:
                        pe.wait_ge(acc_free, 6 * b + (group0[H2, i // GT] if i // GT == h else group0[H1, h]) + 2)
                    for k in range(KD):
                        last = pe.matmul(ring[use % RING][:, lo:GW], proj_t[1][:, k, i * P:(i + 1) * P], proj_t[0][:, k, GW * h + lo:GW * (h + 1)], start=(k == 0), stop=(k == KD - 1))
                    last.then_inc(ring_full, 1)

            def t_tiles(b, h, v):
                pe.wait_ge(work_free, 6 * b + v + 2)
                pe.wait_ge(ring_free, USES * b + use0[f"scores{h}"] + GT * (h + 1) + RING)
                for d in range(GT):
                    pe.wait_ge(masked, 8 * b + GT * h + d + 1)
                    for i in range(GT * h + d + 1):
                        last = pe.matmul(work[d // 2][:, (d % 2) * D:(d % 2 + 1) * D], score_tile(i, d * P, (d + 1) * P), n_rows[:, i, :], start=(i == 0), stop=(i == GT * h + d))
                last.then_inc(work_full, 1)

            def sequence(b, more):
                mlp(b, H1, 0)
                mlp(b, H2, 0)
                score_tiles(b, 0)
                turn(b, R_N1, W_N1, n_rows[:, GT:2 * GT, :])
                t_tiles(b, 0, W_T0)
                mlp(b, H1, 1)
                mlp(b, H2, 1)
                score_tiles(b, 1)
                turn(b, R_M0, W_M0, t_rows)
                t_tiles(b, 1, W_T1)
                mlp(b, FM, 0)
                turn(b, R_M1, W_M1, t_rows)
                mlp(b, FM, 1, more)

            turn(0, R_N0, -1, n_rows[:, 0:GT, :])
            with pe.Fori(0, SEQS - 1) as b:
                sequence(b, True)
            sequence(SEQS - 1, False)


def constants(nc, ctx, outer):
    kit = Kit(nc, ctx, outer, "const")
    sb = kit.sb
    c = {
        "eye": sb("eye", [P, P]), "earlier": sb("earlier", [P, P], bf16), "ones": sb("ones", [P, P], bf16),
        "zeros": sb("zeros", [P, D], bf16), "iota_e": sb("iota_e", [P, EXPERTS], bf16),
        "iota_c": sb("iota_c", [P, CAP], bf16), "partition": sb("partition", [P, 1]), "tile": sb("tile", [P, TILES]),
        "minus_half": sb("minus_half", [P, 2 * GT]),
    }
    filled = kit.sem("filled")
    with ExitStack() as own:
        block = own.enter_context(nc.Block())

        @block.gpsimd
        def _(pool):
            fills = [("eye", 0.0), ("earlier", 1.0), ("ones", 1.0), ("zeros", 0.0), ("minus_half", -0.5)]
            for name, value in fills:
                pool.memset(c[name][:, :], value).then_inc(filled, 1)
            pool.wait_ge(filled, len(fills))
            pool.affine_select(out=c["eye"][:, :], in_=c["eye"][:, :], compare_op=ALU.not_equal, fill=1.0,
                               base=0, pattern=[[-1, P]], channel_multiplier=1).then_inc(filled, 1)
            pool.affine_select(out=c["earlier"][:, :], in_=c["earlier"][:, :], compare_op=ALU.is_gt, fill=0.0,
                               base=0, pattern=[[1, P]], channel_multiplier=-1).then_inc(filled, 1)
            for name, step, n, mult in (("iota_e", 1, EXPERTS, 0), ("iota_c", 1, CAP, 0), ("partition", 1, 1, 1), ("tile", 1, TILES, 0)):
                pool.iota(c[name][:, :], pattern=[[step, n]], base=0, channel_multiplier=mult,
                          allow_small_or_imprecise_dtypes=True).then_inc(filled, 1)
            pool.wait_ge(filled, len(fills) + 6)
    return c


def build(nc, x, w, aw, out):
    with ExitStack() as outer, ExitStack() as ctx:
        xn_d = nc.dram_tensor("xn_rows", (TOKENS, D), fp32, kind="Internal").ap()
        base_d = nc.dram_tensor("base_rows", (TOKENS, D), fp32, kind="Internal").ap()
        y_d = nc.dram_tensor("expert_rows", (SLOTS + 1, D), fp32, kind="Internal").ap()
        consts = constants(nc, ctx, outer)
        kit = Kit(nc, ctx, outer, "routing")
        routing = {"lists": kit.sb("lists", [P, EXPERTS, CH], u32), "slots": kit.sb("slots", [P, TILES, 2], u32),
                   "halves": kit.sb("halves", [P, TILES, 2])}
        x_rows = x.rearrange("b s d -> (b s) d")
        out_rows = out.rearrange("b s d -> (b s) d")
        dispatch(nc, outer, "dispatch0", consts, routing, x_rows, w, xn_d, base_d)
        experts(nc, outer, "experts0", consts, routing, w, xn_d, y_d)
        x2_d = nc.dram_tensor("x2_rows", (TOKENS, D), fp32, kind="Internal").ap()
        attention(nc, outer, "attention", consts, routing, aw, base_d, y_d, x2_d)
        dispatch(nc, outer, "dispatch1", consts, routing, x2_d, w, xn_d, base_d)
        experts(nc, outer, "experts1", consts, routing, w, xn_d, y_d)
        combine(nc, outer, "combine", consts, routing, base_d, y_d, out_rows)


_FFN = ["rms_w", "gate_w", "w13", "w2", "sw_gate", "sw_up", "sw_down"]
_ATTN = ["x", "ln_g", "ln_b"] + [f"{m}_{p}" for m in ("h1", "h2", "fm") for p in ("w1", "b1", "w2", "b2")]


def kernel(**inputs):
    import concourse.bacc as _bacc
    from concourse.bass_utils import run_bass_kernel_spmd as _run

    nc = _bacc.Bacc("TRN2", target_bir_lowering=False, num_devices=1)
    arrays = {}

    def declare(prefix, names):
        aps = {}
        for name in names:
            a = np.ascontiguousarray(inputs[prefix + name])
            arrays[f"in_{prefix}{name}"] = a
            aps[name] = nc.dram_tensor(f"in_{prefix}{name}", a.shape, mybir.dt.from_np(a.dtype), kind="ExternalInput").ap()
        return aps

    aw, w = declare("L0_attn_", _ATTN), declare("L0_ffn_", _FFN)
    out = nc.dram_tensor("out", (SEQS, SEQ, D), fp32, kind="ExternalOutput").ap()
    build(nc, aw["x"], w, aw, out)
    r = _run(nc, [arrays], core_ids=[0])
    return r.results[0]["out"]
```

```python
from contextlib import ExitStack

import concourse.bass as bass
import numpy as np
from concourse import mybir

fp32 = mybir.dt.float32
bf16 = mybir.dt.bfloat16
u32 = mybir.dt.uint32
ALU = mybir.AluOpType
ACT = mybir.ActivationFunctionType
AX = mybir.AxisListType
ds = bass.ds

P = 128
D = 256
KD = D // P
SEQS, SEQ = 8, 1024
TOKENS = SEQS * SEQ
TILES = TOKENS // P
GT = 4
GROUPS = TILES // GT
GW = GT * P
EXPERTS, INNER, CAP = 64, 128, 256
CH = CAP // P
SLOTS = EXPERTS * CAP
LN_EPS, RMS_EPS = 1e-5, 1e-6


class Count:

    def __init__(self, eng, sem, passed):
        self.eng, self.sem, self.passed = eng, sem, passed
        self.total, self.n, self.first = 0, 0, 0

    def enter(self, i, per):
        self.first, self.n, self.per = self.total + i * per, 0, per

    def leave(self, times):
        assert self.n == self.per, (self.n, self.per)
        self.total, self.n, self.first = self.total + times * self.per, 0, self.total + times * self.per

    def tick(self, ins):
        self.n += 1
        ins.then_inc(self.sem, 1)
        return ins

    def settle(self):
        self.eng.wait_ge(self.sem, self.first + self.n)

    def settle_alone(self):
        hold(self.eng, self.sem, self.first + self.n, self.passed)


def hold(eng, sem, value, passed):
    eng.wait_ge(sem, value)
    eng.sem_inc(passed, 1)


def rows(ap, g, tiles=GT):
    v = ap.rearrange("(g t p) n -> g p t n", t=tiles, p=P)
    return v[ds(g, 1), :, :, :].rearrange("a p t n -> p (a t) n")


class Kit:

    def __init__(self, nc, ctx, outer, tag):
        self.nc, self.ctx, self.outer, self.tag = nc, ctx, outer, tag

    def sb(self, name, shape, dt=fp32):
        return self.ctx.enter_context(self.nc.sbuf_tensor(f"{self.tag}_{name}", shape, dt))

    def ps(self, name, shape, dt=fp32):
        return self.ctx.enter_context(self.nc.psum_tensor(f"{self.tag}_{name}", shape, dt))

    def sem(self, name):
        return self.outer.enter_context(self.nc.semaphore(f"{self.tag}_{name}"))


def dispatch(nc, outer, tag, consts, routing, x, w, xn_d, base_d):
    R = 4
    with ExitStack() as ctx:
        kit = Kit(nc, ctx, outer, tag)
        sb, ps, sem = kit.sb, kit.ps, kit.sem
        gate = sb("gate", [P, KD, EXPERTS])
        sw_gate, sw_up = sb("sw_gate", [P, KD, INNER]), sb("sw_up", [P, KD, INNER])
        sw_down = sb("sw_down", [P, D])
        gate_rows = sb("gate_rows", [EXPERTS, D])
        rms_w = sb("rms_w", [P, D])
        x_in = [sb(f"x_in{s}", [P, GT, D]) for s in range(R)]
        xn = [sb(f"xn{s}", [P, GT, D]) for s in range(R)]
        base = [sb(f"base{s}", [P, GT, D]) for s in range(R)]
        xn_t = [sb(f"xn_t{s}", [P, KD, GW]) for s in range(2)]
        silu = [sb(f"silu{s}", [P, GW]) for s in range(2)]
        hidden = [sb(f"hidden{s}", [P, GW]) for s in range(2)]
        stats = [sb(f"stats{s}", [P, GT, 6]) for s in range(2)]
        mean_var = [sb(f"mean_var{s}", [P, GT, 2]) for s in range(2)]
        small = [[sb(f"small{s}_{k}", [P, GT]) for k in range(10)] for s in range(2)]
        logits = [sb(f"logits{s}", [P, GT, EXPERTS]) for s in range(2)]
        top8 = [sb(f"top8_{s}", [P, GT, 8]) for s in range(2)]
        top8_at = [sb(f"top8_at{s}", [P, GT, 8], u32) for s in range(2)]
        chosen = [sb(f"chosen{s}", [P, 2, GT, EXPERTS], bf16) for s in range(2)]
        either = [sb(f"either{s}", [P, GT, EXPERTS], bf16) for s in range(2)]
        before = [sb(f"before{s}", [P, GT, EXPERTS], bf16) for s in range(2)]
        carry = sb("carry", [P, EXPERTS], bf16)
        place_in = sb("place_in", [P, 2, GT, EXPERTS])
        at_place = [sb(f"at_place{s}", [P, 2, GT, CAP], bf16) for s in range(2)]
        token_of = [sb(f"token_of{s}", [P, 2, GT, 2, EXPERTS], bf16) for s in range(2)]
        expert_all, place_all = sb("expert_all", [P, 2, TILES]), sb("place_all", [P, 2, TILES])
        gap_all, late = sb("gap_all", [P, TILES]), sb("late", [P, 2, TILES])
        slot_f = sb("slot_f", [P, 2, TILES])
        list_parts = sb("list_parts", [P, CH, 2, EXPERTS])
        list_f = sb("list_f", [P, CH, EXPERTS])
        ps_t = [ps(f"ps_t{k}", [P, GW]) for k in range(KD)]
        ps_logits = ps_t[0][:, 0:GT * EXPERTS].rearrange("p (t e) -> p t e", t=GT)
        ps_place = ps("ps_place", [P, GT, EXPERTS])
        ps_gate, ps_up = ps("ps_gate", [P, GW]), ps("ps_up", [P, GW])
        ps_down = [ps(f"ps_down{k}", [P, 2, D]) for k in range(2)]
        ps_list = ps("ps_list", [P, CH, 2, EXPERTS])
        ps_list_flat = ps_list[:, :, :, :].rearrange("p c a e -> p (c a e)")

        loaded_w, gate_turned, gate_ready = sem("loaded_w"), sem("gate_turned"), sem("gate_ready")
        x_loaded = [sem(f"x_loaded{s}") for s in range(R)]
        stats_ready, scales_ready, normed_ready = sem("stats_ready"), sem("scales_ready"), sem("normed_ready")
        xn_ready, stored = sem("xn_ready"), [sem(f"stored{s}") for s in range(R)]
        turned, xn_t_ready = sem("turned"), sem("xn_t_ready")
        logits_ready, logits_read = sem("logits_ready"), sem("logits_read")
        gate_up_ready, silu_ready, hidden_ready = sem("gate_up_ready"), sem("silu_ready"), sem("hidden_ready")
        chosen_ready, counts_ready = sem("chosen_ready"), sem("counts_ready")
        places_ready = sem("places_ready")
        at_place_ready, lists_added = sem("at_place_ready"), sem("lists_added")
        down_ready, base_ready = sem("down_ready"), sem("base_ready")
        exp_ready, gap_ready = sem("exp_ready"), sem("gap_ready")
        dve_done, pool_done = sem("dve_done"), sem("pool_done")
        iota_e, iota_c = consts["iota_e"], consts["iota_c"]
        TURNS = (GROUPS - 1) // R
        FIRST_LATE = 1 + R * TURNS

        def in_loop(i, q):
            return R * i + 1 + q, (1 + q) % R, i + (1 + q) // R

        def late_group(g):
            return g, g % R, g // R

        passed = consts["passed"]
        block = ctx.enter_context(nc.Block())

        @block.sync
        def _(sp):
            sp.dma_start(x_in[0][:, :, :], rows(x, 0)).then_inc(x_loaded[0], 16)
            sp.dma_start(rms_w[:, :], w["rms_w"].partition_broadcast(P)).then_inc(loaded_w, 16)
            sp.dma_start(gate_rows[:, :], w["gate_w"]).then_inc(loaded_w, 16)
            sp.dma_start(x_in[1][:, :, :], rows(x, 1)).then_inc(x_loaded[1], 16)
            sp.dma_start(sw_gate[:, :, :], w["sw_gate"].rearrange("(k p) n -> p k n", p=P)).then_inc(loaded_w, 16)
            sp.dma_start(sw_up[:, :, :], w["sw_up"].rearrange("(k p) n -> p k n", p=P)).then_inc(loaded_w, 16)
            sp.dma_start(sw_down[:, :], w["sw_down"]).then_inc(loaded_w, 16)
            for g in range(2, R):
                sp.dma_start(x_in[g][:, :, :], rows(x, g)).then_inc(x_loaded[g], 16)

            def store_xn(g, s):
                sp.wait_ge(xn_ready, g + 1)
                sp.dma_start(rows(xn_d, g), xn[s][:, :, :]).then_inc(stored[s], 16)

            def store_base(g, s):
                sp.wait_ge(base_ready, g + 1)
                sp.dma_start(rows(base_d, g), base[s][:, :, :]).then_inc(stored[s], 16)

            def load_x(g, s):
                sp.wait_ge(normed_ready, g - R + 1)
                sp.dma_start(x_in[s][:, :, :], rows(x, g)).then_inc(x_loaded[s], 16)

            store_xn(0, 0)
            load_x(R, 0)
            with sp.Fori(0, TURNS - 1) as i:
                for q in range(R):
                    g, s, _j = in_loop(i, q)
                    store_xn(g, s)
                    load_x(g + R, s)
                    store_base(g - 1, (s - 1) % R)
            for g in range(R * (TURNS - 1) + 1, GROUPS):
                store_xn(g, g % R)
                if g + R < GROUPS:
                    load_x(g + R, g % R)
                store_base(g - 1, (g - 1) % R)
            store_base(GROUPS - 1, (GROUPS - 1) % R)
            for s in range(R):
                sp.wait_ge(stored[s], 2 * 16 * (GROUPS // R + 1))

        @block.gpsimd
        def _(pool):
            done = Count(pool, pool_done, passed)
            pool.memset(carry[:, :], 0.0).then_inc(pool_done, 1)
            done.total = 1
            pool.wait_ge(loaded_w, 16 * 5)

            def scales(g, s):
                var_eps, r1, ms, ms_eps, r2, a, mn, b, c, d = small[s % 2]
                mean, var = mean_var[s % 2][:, :, 0], mean_var[s % 2][:, :, 1]
                done.settle_alone()
                hold(pool, stats_ready, g + 1, passed)
                done.tick(pool.tensor_scalar(var_eps[:, :], var, LN_EPS, None, ALU.add))
                done.settle()
                done.tick(pool.tensor_tensor(r1[:, :], var_eps[:, :], consts["minus_half"][:, 0:GT], ALU.pow))
                done.settle()
                done.tick(pool.tensor_tensor(ms[:, :], var, r1[:, :], ALU.mult))
                done.tick(pool.tensor_tensor(mn[:, :], mean, r1[:, :], ALU.mult))
                done.settle()
                done.tick(pool.tensor_tensor(ms[:, :], ms[:, :], r1[:, :], ALU.mult))
                done.settle_alone()
                done.tick(pool.tensor_scalar(c[:, :], r1[:, :], 0.5, 1.0, ALU.mult, ALU.add))
                done.tick(pool.tensor_scalar(d[:, :], mn[:, :], -0.5, None, ALU.mult))
                done.tick(pool.tensor_scalar(ms_eps[:, :], ms[:, :], RMS_EPS, None, ALU.add))
                done.settle()
                done.tick(pool.tensor_tensor(r2[:, :], ms_eps[:, :], consts["minus_half"][:, 0:GT], ALU.pow))
                done.settle()
                done.tick(pool.tensor_tensor(a[:, :], r1[:, :], r2[:, :], ALU.mult))
                done.tick(pool.tensor_tensor(b[:, :], mn[:, :], r2[:, :], ALU.mult))
                done.settle_alone()
                pool.tensor_scalar(b[:, :], b[:, :], -1.0, None, ALU.mult).then_inc(scales_ready, 1)

            def weigh(g, s):
                pool.wait_ge(normed_ready, g + 1)
                pool.tensor_tensor(xn[s][:, :, :], xn[s][:, :, :], rms_w[:, :].unsqueeze(1).broadcast_to([P, GT, D]), ALU.mult).then_inc(xn_ready, 1)

            def counts(g, s):
                now, masks = before[s % 2], either[s % 2]
                hold(pool, chosen_ready, g + 1, passed)
                done.settle_alone()
                done.tick(pool.tensor_copy(now[:, 0, :], carry[:, :]))
                for t in range(1, GT):
                    done.settle()
                    done.tick(pool.tensor_tensor(now[:, t, :], now[:, t - 1, :], masks[:, t - 1, :], ALU.add))
                done.settle()
                pool.sem_inc(counts_ready, 1)
                done.tick(pool.tensor_tensor(carry[:, :], now[:, GT - 1, :], masks[:, GT - 1, :], ALU.add))

            SCALES, COUNTS = 11, 5
            done.enter(0, 3 * SCALES + COUNTS)
            for g in range(2):
                scales(g, g)
                weigh(g, g)
            scales(2, 2)
            counts(0, 0)
            weigh(2, 2)
            done.leave(1)
            with pool.Fori(0, TURNS) as i:
                done.enter(i, R * (SCALES + COUNTS))
                for q in range(R):
                    g, s, _j = in_loop(i, q)
                    scales(g + 2, s + 2)
                    counts(g, s)
                    weigh(g + 2, (s + 2) % R)
                done.leave(TURNS)
            done.enter(0, SCALES + 3 * COUNTS)
            for g in range(FIRST_LATE, GROUPS):
                if g + 2 < GROUPS:
                    scales(g + 2, g + 2)
                counts(g, g)
                if g + 2 < GROUPS:
                    weigh(g + 2, (g + 2) % R)
            done.leave(1)
            done.settle()
            pool.sem_inc(passed, 1)

        @block.scalar
        def _(act):
            for s in range(R):
                act.sem_inc(stored[s], 2 * 16)

            def normalise(g, s, j):
                a, b, c, d = (small[s % 2][k] for k in (5, 7, 8, 9))
                act.wait_ge(scales_ready, g + 1)
                act.wait_ge(stored[s % R], 2 * 16 * (j + s // R + 1))
                for t in range(GT):
                    act.activation(base[s % R][:, t, :], x_in[s % R][:, t, :], ACT.Identity, bias=d[:, t:t + 1], scale=c[:, t:t + 1])
                for t in range(GT):
                    last = act.activation(xn[s % R][:, t, :], x_in[s % R][:, t, :], ACT.Identity, bias=b[:, t:t + 1], scale=a[:, t:t + 1])
                last.then_inc(normed_ready, 1)

            def step(g, s, j, ahead=True):
                act.wait_ge(turned, g + 1)
                for k in range(KD):
                    last = act.activation(xn_t[s % 2][:, k, :], ps_t[k][:, :], ACT.Copy)
                last.then_inc(xn_t_ready, 1)
                act.wait_ge(gate_up_ready, g + 1)
                act.activation(silu[s % 2][:, :], ps_gate[:, :], ACT.Silu).then_inc(silu_ready, 1)
                if ahead:
                    normalise(g + 2, s + 2, j)

            normalise(0, 0, 0)
            act.wait_ge(gate_turned, 1)
            act.activation(gate[:, :, :], ps_t[0][:, 0:KD * EXPERTS].rearrange("p (k e) -> p k e", k=KD), ACT.Copy).then_inc(gate_ready, 1)
            normalise(1, 1, 0)
            step(0, 0, 0)
            with act.Fori(0, TURNS) as i:
                for q in range(R):
                    step(*in_loop(i, q))
            for g in range(FIRST_LATE, GROUPS):
                step(*late_group(g), g + 2 < GROUPS)
            act.wait_ge(gap_ready, 1)
            act.activation(gap_all[:, :], gap_all[:, :], ACT.Exp).then_inc(exp_ready, 1)

        @block.vector
        def _(dve):
            done = Count(dve, dve_done, passed)

            def statistics(g, s, j):
                dve.wait_ge(x_loaded[s % R], 16 * (j + s // R + 1))
                for t in range(GT):
                    done.tick(dve.bn_stats(stats[s % 2][:, t, :], x_in[s % R][:, t, :]))
                done.settle_alone()
                for t in range(GT):
                    last = dve.bn_aggr(mean_var[s % 2][:, t, :], stats[s % 2][:, t, :])
                last.then_inc(stats_ready, 1)

            def choose(g, s):
                s = s % 2
                dve.wait_ge(logits_ready, g + 1)
                dve.tensor_copy(logits[s][:, :, :], ps_logits).then_inc(logits_read, 1)
                hold(dve, logits_read, g + 2, passed)
                for t in range(GT):
                    done.tick(dve.max(top8[s][:, t, :], logits[s][:, t, :]))
                done.settle_alone()
                for t in range(GT):
                    done.tick(dve.max_index(top8_at[s][:, t, :], top8[s][:, t, :], logits[s][:, t, :]))
                done.tick(dve.tensor_tensor(gap_all[:, ds(g * GT, GT)], top8[s][:, :, 1], top8[s][:, :, 0], ALU.subtract))
                done.settle_alone()
                done.tick(dve.tensor_copy(expert_all[:, :, ds(g * GT, GT)], top8_at[s][:, :, 0:2].rearrange("p t k -> p k t")))
                done.settle()
                full = [P, 2, GT, EXPERTS]
                done.tick(dve.tensor_tensor(
                    chosen[s][:, :, :, :], iota_e[:, :].unsqueeze(1).unsqueeze(1).broadcast_to(full),
                    expert_all[:, :, ds(g * GT, GT)].unsqueeze(3).broadcast_to(full), ALU.is_equal))
                done.settle()
                dve.tensor_tensor(either[s][:, :, :], chosen[s][:, 0, :, :], chosen[s][:, 1, :, :], ALU.add).then_inc(chosen_ready, 1)
                done.tick(dve.tensor_scalar(token_of[s][:, :, :, 0, :], chosen[s][:, :, :, :], consts["partition"][:, 0:1], None, ALU.mult))
                done.tick(dve.tensor_tensor(
                    token_of[s][:, :, :, 1, :], chosen[s][:, :, :, :],
                    consts["tile"][:, ds(g * GT, GT)].unsqueeze(1).unsqueeze(3).broadcast_to(full), ALU.mult))

            def shared_hidden(g, s):
                dve.wait_ge(silu_ready, g + 1)
                dve.tensor_tensor(hidden[s % 2][:, :], silu[s % 2][:, :], ps_up[:, :], ALU.mult).then_inc(hidden_ready, 1)

            def places(g, s):
                s = s % 2
                dve.wait_ge(places_ready, g + 1)
                done.tick(dve.tensor_tensor(place_in[:, :, :, :], chosen[s][:, :, :, :], ps_place[:, :, :].unsqueeze(1).broadcast_to([P, 2, GT, EXPERTS]), ALU.mult))
                done.settle_alone()
                done.tick(dve.tensor_reduce(place_all[:, :, ds(g * GT, GT)], place_in[:, :, :, :], AX.X, ALU.add))
                done.settle()
                for k in range(2):
                    for t in range(GT):
                        last = dve.tensor_scalar(at_place[s][:, k, t, :], iota_c[:, :], place_all[:, k, ds(g * GT + t, 1)], None, ALU.is_equal)
                last.then_inc(at_place_ready, 1)

            def add_shared(g, s):
                dve.wait_ge(down_ready, g + 1)
                for k in range(2):
                    half = base[s][:, 2 * k:2 * k + 2, :]
                    last = dve.scalar_tensor_tensor(half, ps_down[k][:, :, :], 0.5, half, ALU.mult, ALU.add)
                last.then_inc(base_ready, 1)

            def step(g, s, j, ahead=True, behind=True):
                if ahead:
                    hold(dve, scales_ready, g + 1, passed)
                    statistics(g + 2, s + 2, j)
                if behind:
                    add_shared(g - 1, (s - 1) % R)
                    places(g - 1, s + 1)
                choose(g, s)
                shared_hidden(g, s)

            STATS, CHOOSE, PLACES = GT, 2 * GT + 5, 2
            done.enter(0, 3 * STATS + CHOOSE)
            statistics(0, 0, 0)
            statistics(1, 1, 0)
            step(0, 0, 0, behind=False)
            done.leave(1)
            with dve.Fori(0, TURNS) as i:
                done.enter(i, R * (STATS + CHOOSE + PLACES))
                for q in range(R):
                    step(*in_loop(i, q))
                done.leave(TURNS)
            done.enter(0, STATS + 3 * CHOOSE + 4 * PLACES)
            for g in range(FIRST_LATE, GROUPS):
                step(*late_group(g), ahead=g + 2 < GROUPS)
            add_shared(GROUPS - 1, (GROUPS - 1) % R)
            places(GROUPS - 1, GROUPS - 1)
            done.leave(1)
            done.settle()
            dve.sem_inc(gap_ready, 1)

            def last(ins):
                done.tick(ins)
                done.settle()

            done.tick(dve.tensor_scalar(late[:, :, :], place_all[:, :, :], float(CAP), float(2 * SLOTS), ALU.is_ge, ALU.mult))
            last(dve.scalar_tensor_tensor(slot_f[:, :, :], expert_all[:, :, :], float(CAP), place_all[:, :, :], ALU.mult, ALU.add))
            last(dve.tensor_tensor(slot_f[:, :, :], slot_f[:, :, :], late[:, :, :], ALU.add))
            last(dve.tensor_scalar(slot_f[:, :, :], slot_f[:, :, :], float(SLOTS), None, ALU.min))
            last(dve.tensor_copy(routing["slots"][:, :, :], slot_f[:, :, :].rearrange("p k t -> p t k")))
            dve.wait_ge(exp_ready, 1)
            last(dve.tensor_scalar(late[:, 0, :], gap_all[:, :], 1.0, None, ALU.add))
            last(dve.reciprocal(late[:, 0, :], late[:, 0, :]))
            last(dve.tensor_scalar(routing["halves"][:, :, 0], late[:, 0, :], 0.5, None, ALU.mult))
            last(dve.tensor_tensor(routing["halves"][:, :, 1], routing["halves"][:, :, 0], gap_all[:, :], ALU.mult))
            dve.wait_ge(lists_added, GROUPS + 1)
            last(dve.tensor_copy(list_parts[:, :, :, :], ps_list[:, :, :, :]))
            last(dve.scalar_tensor_tensor(list_f[:, :, :], list_parts[:, :, 1, :], float(P), list_parts[:, :, 0, :], ALU.mult, ALU.add))
            last(dve.tensor_copy(routing["lists"][:, :, :], list_f[:, :, :].rearrange("p c e -> p e c")))

        @block.tensor
        def _(pe):
            zeros = consts["zeros"]
            pe.wait_ge(loaded_w, 16 * 5)
            for k in range(KD):
                last = pe.transpose(ps_t[0][:, k * EXPERTS:(k + 1) * EXPERTS], gate_rows[:, k * P:(k + 1) * P], consts["eye"][0:EXPERTS, 0:EXPERTS])
            last.then_inc(gate_turned, 1)
            pe.matmul(ps_list_flat, zeros[:, 0:P], zeros[:, :], start=True, stop=False)
            pe.wait_ge(gate_ready, 1)
            pe.sem_inc(logits_read, 1)

            def turn(g, s):
                pe.wait_ge(xn_ready, g + 1)
                pe.wait_ge(logits_read, g + 1)
                for k in range(KD):
                    for t in range(GT):
                        last = pe.transpose(ps_t[k][:, t * P:(t + 1) * P], xn[s][:, t, k * P:(k + 1) * P], consts["eye"][:, :])
                last.then_inc(turned, 1)

            def down(g, s):
                pe.wait_ge(hidden_ready, g + 1)
                for t in range(GT):
                    last = pe.matmul(ps_down[t // 2][:, t % 2, :], hidden[s % 2][:, t * P:(t + 1) * P], sw_down[:, :], start=True, stop=True)
                last.then_inc(down_ready, 1)

            def places(g, s):
                pe.wait_ge(counts_ready, g + 1)
                for t in range(GT):
                    pe.matmul(ps_place[:, t, :], consts["earlier"][:, :], either[s % 2][:, t, :], start=True, stop=False)
                    last = pe.matmul(ps_place[:, t, :], consts["ones"][:, :], before[s % 2][:, t, :], start=False, stop=True)
                last.then_inc(places_ready, 1)

            def router(g, s):
                pe.wait_ge(xn_t_ready, g + 1)
                for t in range(GT):
                    for k in range(KD):
                        last = pe.matmul(ps_logits[:, t, :], xn_t[s % 2][:, k, t * P:(t + 1) * P], gate[:, k, :], start=(k == 0), stop=(k == KD - 1))
                last.then_inc(logits_ready, 1)

            def gate_up(g, s):
                for wt, out in ((sw_gate, ps_gate), (sw_up, ps_up)):
                    for k in range(KD):
                        last = pe.matmul(out[:, :], wt[:, k, :], xn_t[s % 2][:, k, :], start=(k == 0), stop=(k == KD - 1))
                last.then_inc(gate_up_ready, 1)

            def lists(g, s):
                pe.wait_ge(at_place_ready, g + 1)
                for k in range(2):
                    for t in range(GT):
                        for c in range(CH):
                            last = pe.matmul(
                                ps_list[:, c, :, :], at_place[s % 2][:, k, t, c * P:(c + 1) * P], token_of[s % 2][:, k, t, :, :],
                                start=False, stop=False, skip_group_check=True)
                last.then_inc(lists_added, 1)

            def step(g, s, _j):
                turn(g, s)
                down(g - 1, s + 1)
                places(g - 1, s + 1)
                router(g, s)
                gate_up(g, s)
                lists(g - 1, s + 1)

            turn(0, 0)
            router(0, 0)
            gate_up(0, 0)
            with pe.Fori(0, TURNS) as i:
                for q in range(R):
                    step(*in_loop(i, q))
            for g in range(FIRST_LATE, GROUPS):
                step(*late_group(g))
            down(GROUPS - 1, GROUPS - 1)
            places(GROUPS - 1, GROUPS - 1)
            lists(GROUPS - 1, GROUPS - 1)
            pe.matmul(ps_list_flat, zeros[:, 0:P], zeros[:, :], start=False, stop=True).then_inc(lists_added, 1)


def experts(nc, outer, tag, consts, routing, w, xn_d, y_d):
    R = 4
    TURNS = EXPERTS // R - 1
    with ExitStack() as ctx:
        kit = Kit(nc, ctx, outer, tag)
        sb, ps, sem = kit.sb, kit.ps, kit.sem
        w13 = [sb(f"w13_{s}", [P, KD, 2 * INNER]) for s in range(R)]
        w2 = [sb(f"w2_{s}", [P, D]) for s in range(R)]
        who = [sb(f"who{s}", [P, CH], u32) for s in range(R)]
        xg = [sb(f"xg{s}", [P, CH, D]) for s in range(R)]
        xg_t = [sb(f"xg_t{s}", [P, KD, CAP]) for s in range(R)]
        silu = [sb(f"silu{s}", [P, CAP]) for s in range(R)]
        hidden = [sb(f"hidden{s}", [P, CAP]) for s in range(R)]
        y = [sb(f"y{s}", [P, CH, D]) for s in range(R)]
        zero_row = sb("zero_row", [1, D])
        ps_t = [ps(f"ps_t{s}", [P, KD, CAP]) for s in range(2)]
        ps_gu = [ps(f"ps_gu{s}", [P, 2, CAP]) for s in range(2)]
        ps_y = [ps(f"ps_y{s}", [P, CH, D]) for s in range(2)]

        w_loaded = [sem(f"w_loaded{s}") for s in range(R)]
        rows_loaded = [sem(f"rows_loaded{s}") for s in range(R)]
        y_stored = [sem(f"y_stored{s}") for s in range(R)]
        zero_filled, zero_stored = sem("zero_filled"), sem("zero_stored")
        turned, xg_t_ready, gate_up_ready = sem("turned"), sem("xg_t_ready"), sem("gate_up_ready")
        silu_ready, hidden_ready, y_ready, y_copied = sem("silu_ready"), sem("hidden_ready"), sem("y_ready"), sem("y_copied")
        pool_done = sem("pool_done")

        passed = consts["passed"]
        block = ctx.enter_context(nc.Block())

        @block.sync
        def _(sp):
            def load(e, s):
                sp.dma_start(w13[s][:, :, :], w["w13"][ds(e, 1), :, :].rearrange("a (k p) f -> p (a k) f", p=P)).then_inc(w_loaded[s], 16)
                sp.dma_start(w2[s][:, :], w["w2"][ds(e, 1), :, :].rearrange("a p h -> p (a h)")).then_inc(w_loaded[s], 16)

            def store(e, s):
                sp.wait_ge(y_copied, e + 3)
                out = y_d[0:SLOTS, :].rearrange("(e c p) h -> e p c h", p=P, c=CH)
                sp.dma_start(out[ds(e, 1), :, :, :].rearrange("a p c h -> p (a c) h"), y[s][:, :, :]).then_inc(y_stored[s], 16)

            for s in range(R):
                load(s, s)
            sp.wait_ge(zero_filled, 1)
            sp.dma_start(y_d[SLOTS:SLOTS + 1, :], zero_row[0:1, :]).then_inc(zero_stored, 16)
            with sp.Fori(0, TURNS) as i:
                for s in range(R):
                    e = R * i + s
                    store(e, s)
                    load(e + R, s)
            for s in range(R):
                store(EXPERTS - R + s, s)
            for s in range(R):
                sp.wait_ge(y_stored[s], 16 * (EXPERTS // R + 1))
            sp.wait_ge(zero_stored, 16)

        @block.gpsimd
        def _(pool):
            with pool.Fori(0, EXPERTS // R) as i:
                for s in range(R):
                    e = R * i + s
                    hold(pool, turned, e + 1, passed)
                    pool.tensor_copy(who[s][:, :], routing["lists"][:, ds(e, 1), :].rearrange("p a c -> p (a c)")).then_inc(pool_done, 1)
                    hold(pool, pool_done, e + 1, passed)
                    for c in range(CH):
                        pool.indirect_dma_start(
                            out=xg[s][:, c, :], out_offset=None, in_=xn_d,
                            in_offset=bass.IndirectOffsetOnAxis(ap=who[s][:, c:c + 1], axis=0),
                        ).then_inc(rows_loaded[s], 16)

        @block.scalar
        def _(act):
            def copy_turned(e, s):
                act.wait_ge(turned, e + 1 + R)
                act.activation(xg_t[s % R][:, :, :], ps_t[s % 2][:, :, :], ACT.Copy).then_inc(xg_t_ready, 1)

            def gate(e, s):
                act.wait_ge(gate_up_ready, e + 1)
                act.activation(silu[s][:, :], ps_gu[s % 2][:, 0, :], ACT.Silu).then_inc(silu_ready, 1)

            copy_turned(0, 0)
            with act.Fori(0, TURNS) as i:
                for s in range(R):
                    copy_turned(R * i + s + 1, s + 1)
                    gate(R * i + s, s)
            for s in range(R):
                if s + 1 < R:
                    copy_turned(EXPERTS - R + s + 1, s + 1)
                gate(EXPERTS - R + s, s)

        @block.vector
        def _(dve):
            dve.memset(zero_row[:, :], 0.0).then_inc(zero_filled, 1)
            for s in range(R):
                dve.sem_inc(y_stored[s], 16)
            with dve.Fori(0, EXPERTS // R) as i:
                for s in range(R):
                    e = R * i + s
                    dve.wait_ge(silu_ready, e + 1)
                    dve.tensor_tensor(hidden[s][:, :], silu[s][:, :], ps_gu[s % 2][:, 1, :], ALU.mult).then_inc(hidden_ready, 1)
                    dve.wait_ge(y_ready, e + 1)
                    dve.wait_ge(y_stored[s], 16 * (i + 1))
                    dve.tensor_copy(y[s][:, :, :], ps_y[s % 2][:, :, :]).then_inc(y_copied, 1)

        @block.tensor
        def _(pe):
            pe.sem_inc(turned, R)
            pe.sem_inc(y_copied, 2)

            def turn(e, s, i):
                pe.wait_ge(rows_loaded[s % R], 2 * 16 * (i + s // R + 1))
                for k in range(KD):
                    for c in range(CH):
                        last = pe.transpose(ps_t[s % 2][:, k, c * P:(c + 1) * P], xg[s % R][:, c, k * P:(k + 1) * P], consts["eye"][:, :])
                last.then_inc(turned, 1)

            def gate_up(e, s, i):
                pe.wait_ge(xg_t_ready, e + 1)
                pe.wait_ge(w_loaded[s % R], 2 * 16 * (i + s // R + 1))
                for half in range(2):
                    for k in range(KD):
                        last = pe.matmul(ps_gu[s % 2][:, half, :], w13[s % R][:, k, half * INNER:(half + 1) * INNER], xg_t[s % R][:, k, :], start=(k == 0), stop=(k == KD - 1))
                last.then_inc(gate_up_ready, 1)

            def down(e, s):
                pe.wait_ge(hidden_ready, e + 1)
                pe.wait_ge(y_copied, e + 1)
                for c in range(CH):
                    last = pe.matmul(ps_y[s % 2][:, c, :], hidden[s][:, c * P:(c + 1) * P], w2[s][:, :], start=True, stop=True)
                last.then_inc(y_ready, 1)

            turn(0, 0, 0)
            turn(1, 1, 0)
            gate_up(0, 0, 0)
            with pe.Fori(0, TURNS) as i:
                for s in range(R):
                    e = R * i + s
                    turn(e + 2, s + 2, i)
                    gate_up(e + 1, s + 1, i)
                    down(e, s)
            for s in range(R):
                e = EXPERTS - R + s
                if s + 2 < R:
                    turn(e + 2, s + 2, TURNS)
                if s + 1 < R:
                    gate_up(e + 1, s + 1, TURNS)
                down(e, s)


def combine(nc, outer, tag, consts, routing, base_d, y_d, out):
    with ExitStack() as ctx:
        kit = Kit(nc, ctx, outer, tag)
        sb, sem = kit.sb, kit.sem
        R = 4
        acc = [sb(f"acc{s}", [P, GT, D]) for s in range(R)]
        ye = [sb(f"ye{s}", [P, GT, 2, D]) for s in range(R)]
        where = [sb(f"where{s}", [P, GT, 2], u32) for s in range(R)]
        half = [sb(f"half{s}", [P, GT, 2]) for s in range(R)]
        base_loaded, rows_loaded = [sem(f"base_loaded{s}") for s in range(R)], [sem(f"rows_loaded{s}") for s in range(R)]
        stored = [sem(f"stored{s}") for s in range(R)]
        added, added_rows, pool_done, dve_done = sem("added"), sem("added_rows"), sem("pool_done"), sem("dve_done")
        passed = consts["passed"]
        block = ctx.enter_context(nc.Block())

        @block.sync
        def _(sp):
            for s in range(R):
                sp.dma_start(acc[s][:, :, :], rows(base_d, s)).then_inc(base_loaded[s], 16)
            with sp.Fori(0, GROUPS // R - 1) as i:
                for s in range(R):
                    g = R * i + s
                    sp.wait_ge(added, g + 1)
                    sp.dma_start(rows(out, g), acc[s][:, :, :]).then_inc(stored[s], 16)
                    sp.wait_ge(stored[s], 16 * (i + 1))
                    sp.dma_start(acc[s][:, :, :], rows(base_d, g + R)).then_inc(base_loaded[s], 16)
            for s in range(R):
                sp.wait_ge(added, GROUPS - R + s + 1)
                sp.dma_start(rows(out, GROUPS - R + s), acc[s][:, :, :]).then_inc(stored[s], 16)
            for s in range(R):
                sp.wait_ge(stored[s], 16 * (GROUPS // R))

        @block.gpsimd
        def _(pool):
            pool.sem_inc(added_rows, R)
            with pool.Fori(0, GROUPS // R) as i:
                for s in range(R):
                    g = R * i + s
                    hold(pool, added_rows, g + 1, passed)
                    pool.tensor_copy(where[s][:, :, :], routing["slots"][:, ds(g * GT, GT), :]).then_inc(pool_done, 1)
                    hold(pool, pool_done, g + 1, passed)
                    for t in range(GT):
                        for k in range(2):
                            pool.indirect_dma_start(
                                out=ye[s][:, t, k, :], out_offset=None, in_=y_d,
                                in_offset=bass.IndirectOffsetOnAxis(ap=where[s][:, t, k:k + 1], axis=0),
                            ).then_inc(rows_loaded[s], 16)

        @block.vector
        def _(dve):
            done = Count(dve, dve_done, passed)
            with dve.Fori(0, GROUPS // R) as i:
                done.enter(i, R * (1 + 2 * GT))
                for s in range(R):
                    g = R * i + s
                    done.tick(dve.tensor_copy(half[s][:, :, :], routing["halves"][:, ds(g * GT, GT), :]))
                    done.settle()
                    dve.wait_ge(base_loaded[s], 16 * (i + 1))
                    dve.wait_ge(rows_loaded[s], 16 * 2 * GT * (i + 1))
                    for k in range(2):
                        for t in range(GT):
                            done.tick(dve.scalar_tensor_tensor(acc[s][:, t, :], ye[s][:, t, k, :], half[s][:, t, k:k + 1], acc[s][:, t, :], ALU.mult, ALU.add))
                        done.settle()
                    dve.sem_inc(added, 1)
                    dve.sem_inc(added_rows, 1)
                done.leave(GROUPS // R)


def attention(nc, outer, tag, consts, routing, w, base_d, y_d, x2_d):
    fr = mybir.dt.float32r
    FC = 1024 // P
    RING, GELUS, PARTS, LAG = 4, 2, 3, 2
    H1, H2, FM = range(3)
    CHUNKS = 6 * FC
    USES = CHUNKS + 3 * GT
    chunk0 = {(H1, 0): 0, (H2, 0): FC, (H1, 1): 2 * FC, (H2, 1): 3 * FC, (FM, 0): 4 * FC, (FM, 1): 5 * FC}
    use0 = {(H1, 0): 0, (H2, 0): FC, "scores0": 2 * FC, (H1, 1): 2 * FC + GT, (H2, 1): 3 * FC + GT,
            "scores1": 4 * FC + GT, (FM, 0): 4 * FC + 3 * GT, (FM, 1): 5 * FC + 3 * GT}
    group0 = {(H1, 0): 0, (H2, 0): 1, (H1, 1): 2, (H2, 1): 3, (FM, 0): 4, (FM, 1): 5}
    W_N1, W_T0, W_M0, W_T1, W_M1, W_N0_NEXT = range(6)
    R_N0, R_N1, R_M0, R_M1 = range(4)
    S_N0, S_N1, S_T0, S_M0, S_T1, S_M1 = range(6)
    with ExitStack() as ctx:
        kit = Kit(nc, ctx, outer, tag)
        sb, ps, sem = kit.sb, kit.ps, kit.sem
        w1 = [[sb(f"w1_{m}_{part}", [P, KD, FC * P], fr) for part in "hl"] for m in range(3)]
        w2 = [[sb(f"w2_{m}_{part}", [P, FC, D], fr) for part in "hl"] for m in range(3)]
        b1 = sb("b1", [P, 3, FC])
        b2 = sb("b2", [P, 2, KD])
        g_row, b_row, b2_row = sb("g_row", [P, D]), sb("b_row", [P, D]), sb("b2_row", [P, D])
        rows_t = [[sb(f"rows_t{h}_{part}", [P, KD, GW], fr) for part in "hl"] for h in range(2)]
        gelu = [sb(f"gelu{j}", [P, GW]) for j in range(GELUS)]
        hid = [[sb(f"hid{j}_{part}", [P, GW], fr) for part in "hl"] for j in range(PARTS)]
        proj_t = [sb(f"proj_t{m}", [P, KD, SEQ]) for m in range(2)]
        score_at = [GW * i for i in range(GT)] + [GT * GW + sum(GW - P * e for e in range(d)) for d in range(GT)]
        scores = sb("scores", [P, score_at[-1] + P])
        n_rows = sb("n_rows", [P, 2 * GT, D])
        x1, z = sb("x1", [P, 2 * GT, D]), sb("z", [P, 2 * GT, D])
        base_in = sb("base_in", [P, GT, D])
        ye = sb("ye", [P, GT, 2, D])
        where, half = sb("where", [P, GT, 2], u32), sb("half", [P, GT, 2])
        t_rows = sb("t_rows", [P, GT, D])
        stats, mean_var = sb("stats", [P, GT, 6]), sb("mean_var", [P, GT, 2])
        var_eps, r1, var_z, r2, rr = [sb(f"small{k}", [P, GT]) for k in range(5)]
        ring = [ps(f"ring{j}", [P, GW]) for j in range(RING)]
        acc = [ps(f"acc{j}", [P, GW]) for j in range(2)]
        work = [ps(f"work{j}", [P, GW]) for j in range(2)]

        w_loaded, w_rounded, w_split = [sem(f"w_loaded{j}") for j in range(4)], sem("w_rounded"), sem("w_split")
        b_loaded = sem("b_loaded")
        base_loaded, rows_loaded, rows_used, x_stored = sem("base_loaded"), sem("rows_loaded"), sem("rows_used"), sem("x_stored")
        ring_full, ring_free = sem("ring_full"), sem("ring_free")
        hid_ready, hid_used = sem("hid_ready"), sem("hid_used")
        acc_free = sem("acc_free")
        work_full, work_free = sem("work_full"), sem("work_free")
        hi_ready, turned_ready = sem("hi_ready"), sem("turned_ready")
        masked, rows_ready = sem("masked"), sem("rows_ready")
        stats_ready, scales_ready, sums_ready = sem("stats_ready"), sem("scales_ready"), sem("sums_ready")
        out_ready = sem("out_ready")
        dve_done, pool_done = sem("dve_done"), sem("pool_done")
        staging = [a[:, :, :].rearrange("p a b -> p (a b)") for a in (proj_t[0], proj_t[1], x1, z)]
        names = ("h1", "h2", "fm")

        def score_tile(i, lo, hi):
            start = score_at[i] - (i - GT) * P if i >= GT else score_at[i]
            return scores[:, start + lo:start + hi]

        passed = consts["passed"]
        block = ctx.enter_context(nc.Block())

        @block.sync
        def _(sp):
            for m, name in enumerate(names):
                for j, (part, form, size) in enumerate((("_w1", "(k p) f -> p k f", KD), ("_w2", "(c p) d -> p c d", FC))):
                    n = 2 * m + j
                    if n >= len(staging):
                        sp.wait_ge(w_split, n - len(staging) + 1)
                    at = n % len(staging)
                    sp.dma_start(staging[at].rearrange("p (a b) -> p a b", a=size), w[name + part].rearrange(form, p=P)).then_inc(w_loaded[at], 16)
                if m == 0:
                    sp.dma_start(base_in[:, :, :], rows(base_d, 0)).then_inc(base_loaded, 16)
                    for j, n2 in enumerate(names):
                        sp.dma_start(b1[:, j, :], w[n2 + "_b1"].rearrange("(c p) -> p c", p=P), allow_slow_non_contiguous=True).then_inc(b_loaded, 16)
                    for j, n2 in enumerate(names[:2]):
                        sp.dma_start(b2[:, j, :], w[n2 + "_b2"].rearrange("(k p) -> p k", p=P), allow_slow_non_contiguous=True).then_inc(b_loaded, 16)
                    for row, n2 in ((g_row, "ln_g"), (b_row, "ln_b"), (b2_row, "fm_b2")):
                        sp.dma_start(row[:, :], w[n2].partition_broadcast(P)).then_inc(b_loaded, 16)

            def load_base(g):
                sp.wait_ge(rows_used, g + 1)
                sp.dma_start(base_in[:, :, :], rows(base_d, g)).then_inc(base_loaded, 16)

            def store(b, h):
                sp.wait_ge(out_ready, 2 * b + h + 1)
                sp.dma_start(rows(x2_d, 2 * b + h), x1[:, GT * h:GT * (h + 1), :]).then_inc(x_stored, 16)

            load_base(1)
            with sp.Fori(0, SEQS - 1) as b:
                load_base(2 * b + 2)
                store(b, 0)
                load_base(2 * b + 3)
                store(b, 1)
            store(SEQS - 1, 0)
            store(SEQS - 1, 1)
            sp.wait_ge(x_stored, 16 * (2 * SEQS + 2))

        @block.gpsimd
        def _(pool):
            done = Count(pool, pool_done, passed)
            pool.sem_inc(rows_used, 1)
            pool.wait_ge(b_loaded, 16 * 8)

            def gather(b, h):
                g = 2 * b + h
                hold(pool, rows_used, g + 1, passed)
                done.settle_alone()
                done.tick(pool.tensor_copy(where[:, :, :], routing["slots"][:, ds(g * GT, GT), :]))
                done.settle_alone()
                for t in range(GT):
                    for k in range(2):
                        pool.indirect_dma_start(
                            out=ye[:, t, k, :], out_offset=None, in_=y_d,
                            in_offset=bass.IndirectOffsetOnAxis(ap=where[:, t, k:k + 1], axis=0),
                        ).then_inc(rows_loaded, 16)

            def scales(b, order, twice):
                hold(pool, stats_ready, 6 * b + order + 1, passed)
                var = mean_var[:, :, 1]
                done.tick(pool.tensor_scalar(var_eps[:, :], var, LN_EPS, None, ALU.add))
                done.settle()
                done.tick(pool.tensor_tensor(r1[:, :], var_eps[:, :], consts["minus_half"][:, 0:GT], ALU.pow))
                if twice:
                    done.settle()
                    done.tick(pool.tensor_tensor(var_z[:, :], var, r1[:, :], ALU.mult))
                    done.settle()
                    done.tick(pool.tensor_tensor(var_z[:, :], var_z[:, :], r1[:, :], ALU.mult))
                    done.settle_alone()
                    done.tick(pool.tensor_scalar(var_z[:, :], var_z[:, :], LN_EPS, None, ALU.add))
                    done.settle()
                    done.tick(pool.tensor_tensor(r2[:, :], var_z[:, :], consts["minus_half"][:, 0:GT], ALU.pow))
                    done.settle()
                    done.tick(pool.tensor_tensor(rr[:, :], r1[:, :], r2[:, :], ALU.mult))
                done.settle()
                pool.sem_inc(scales_ready, 1)

            def sums(b, h):
                xs, zs = x1[:, GT * h:GT * (h + 1), :], z[:, GT * h:GT * (h + 1), :]
                pool.wait_ge(rows_ready, 4 * b + h + 1)
                done.tick(pool.tensor_tensor(xs, xs, zs, ALU.add))
                done.settle()
                done.tick(pool.tensor_tensor(xs, xs, b2_row[:, :].unsqueeze(1).broadcast_to([P, GT, D]), ALU.add))
                done.tick(pool.tensor_tensor(zs, zs, b_row[:, :].unsqueeze(1).broadcast_to([P, GT, D]), ALU.add))
                done.settle()
                pool.sem_inc(sums_ready, 1)

            def mask(b, h):
                for d in range(GT):
                    i = GT * h + d
                    hold(pool, ring_free, USES * b + use0[f"scores{h}"] + i + RING + 1, passed)
                    tile = score_tile(i, d * P, (d + 1) * P)
                    pool.affine_select(out=tile, in_=tile, compare_op=ALU.is_ge, fill=0.0, base=0,
                                       pattern=[[1, P]], channel_multiplier=-1).then_inc(masked, 1)

            def sequence(b, more):
                scales(b, S_N1, True)
                if more:
                    gather(b + 1, 0)
                sums(b, 1)
                mask(b, 0)
                scales(b, S_T0, False)
                scales(b, S_M0, False)
                mask(b, 1)
                scales(b, S_T1, False)
                scales(b, S_M1, False)
                if more:
                    scales(b + 1, S_N0, True)
                    gather(b + 1, 1)
                    sums(b + 1, 0)

            done.enter(0, 12)
            gather(0, 0)
            scales(0, S_N0, True)
            gather(0, 1)
            sums(0, 0)
            done.leave(1)
            with pool.Fori(0, SEQS - 1) as b:
                done.enter(b, 2 * 7 + 4 * 2 + 2 * 3 + 2)
                sequence(b, True)
                done.leave(SEQS - 1)
            done.enter(0, 7 + 4 * 2 + 3)
            sequence(SEQS - 1, False)
            done.leave(1)

        @block.scalar
        def _(act):
            act.sem_inc(ring_free, RING)
            act.sem_inc(work_free, 1)
            for n in range(6):
                hi = (w1, w2)[n % 2][n // 2][0][:, :, :].rearrange("p a b -> p (a b)")
                act.wait_ge(w_loaded[n % len(staging)], 16 * (n // len(staging) + 1))
                act.activation(hi, staging[n % len(staging)], ACT.Copy).then_inc(w_rounded, 1)
            act.wait_ge(b_loaded, 16 * 8)

            def mlp_chunk(b, m, h, c):
                n = CHUNKS * b + chunk0[m, h] + c
                j = (chunk0[m, h] + c)
                act.wait_ge(ring_full, USES * b + use0[m, h] + c + 1)
                act.wait_ge(hid_used, n + 1)
                act.wait_ge(hid_ready, n + 1)
                src = ring[(use0[m, h] + c) % RING][:, :]
                act.activation(hid[j % PARTS][0][:, :], src, ACT.Gelu, bias=b1[:, m, c:c + 1])
                act.activation(gelu[j % GELUS][:, :], src, ACT.Gelu, bias=b1[:, m, c:c + 1]).then_inc(ring_free, 1)

            def score_tiles(b, h):
                for i in range(GT * (h + 1)):
                    lo = max(i - GT * h, 0) * P
                    use = use0[f"scores{h}"] + i
                    act.wait_ge(ring_full, USES * b + use + 1)
                    act.activation(score_tile(i, lo, GW), ring[use % RING][:, lo:GW], ACT.Copy).then_inc(ring_free, 1)

            def turned_hi(b, v, h):
                act.wait_ge(work_full, 6 * b + v + 2)
                for k in range(KD):
                    last = act.activation(rows_t[h][0][:, k, :], work[k][:, :], ACT.Copy)
                last.then_inc(hi_ready, 1)

            def t_gelu(b, v, h):
                act.wait_ge(work_full, 6 * b + v + 2)
                for j in range(2):
                    last = act.activation(t_rows[:, 2 * j:2 * j + 2, :], work[j][:, :].rearrange("p (t d) -> p t d", t=2), ACT.Gelu)
                last.then_inc(work_free, 1)

            def sequence(b, more):
                for m in (H1, H2):
                    for c in range(FC):
                        mlp_chunk(b, m, 0, c)
                score_tiles(b, 0)
                turned_hi(b, W_N1, 1)
                t_gelu(b, W_T0, 0)
                for m in (H1, H2):
                    for c in range(FC):
                        mlp_chunk(b, m, 1, c)
                score_tiles(b, 1)
                turned_hi(b, W_M0, 0)
                t_gelu(b, W_T1, 1)
                for c in range(FC):
                    mlp_chunk(b, FM, 0, c)
                turned_hi(b, W_M1, 1)
                for c in range(FC):
                    if c == FC - 1 and more:
                        turned_hi(b, W_N0_NEXT, 0)
                    mlp_chunk(b, FM, 1, c)

            turned_hi(0, -1, 0)
            with act.Fori(0, SEQS - 1) as b:
                sequence(b, True)
            sequence(SEQS - 1, False)

        @block.vector
        def _(dve):
            done = Count(dve, dve_done, passed)
            dve.sem_inc(hid_ready, GELUS)
            dve.sem_inc(acc_free, 1)
            dve.sem_inc(x_stored, 2 * 16)
            for n in range(6):
                hi, lo = [part[:, :, :].rearrange("p a b -> p (a b)") for part in (w1, w2)[n % 2][n // 2]]
                dve.wait_ge(w_rounded, n + 1)
                dve.tensor_tensor(lo, staging[n % len(staging)], hi.bitcast(fp32), ALU.subtract).then_inc(w_split, 1)
            dve.wait_ge(w_split, 6)
            dve.wait_ge(b_loaded, 16 * 8)

            def add_rows(b, h):
                g = 2 * b + h
                done.tick(dve.tensor_copy(half[:, :, :], routing["halves"][:, ds(g * GT, GT), :]))
                done.settle()
                dve.wait_ge(x_stored, 16 * (g + 1))
                dve.wait_ge(base_loaded, 16 * (g + 1))
                dve.wait_ge(rows_loaded, 16 * 2 * GT * (g + 1))
                for t in range(GT):
                    done.tick(dve.scalar_tensor_tensor(x1[:, GT * h + t, :], ye[:, t, 0, :], half[:, t, 0:1], base_in[:, t, :], ALU.mult, ALU.add))
                done.settle()
                for t in range(GT):
                    done.tick(dve.scalar_tensor_tensor(x1[:, GT * h + t, :], ye[:, t, 1, :], half[:, t, 1:2], x1[:, GT * h + t, :], ALU.mult, ALU.add))
                done.settle()
                dve.sem_inc(rows_used, 1)

            def statistics(src):
                for t in range(GT):
                    done.tick(dve.bn_stats(stats[:, t, :], src[:, t, :]))
                done.settle_alone()
                for t in range(GT):
                    done.tick(dve.bn_aggr(mean_var[:, t, :], stats[:, t, :]))
                done.settle()
                dve.sem_inc(stats_ready, 1)

            def centred(dst, src):
                for t in range(GT):
                    done.tick(dve.scalar_tensor_tensor(dst[:, t, :], src[:, t, :], mean_var[:, t, 0:1], g_row[:, :], ALU.subtract, ALU.mult))
                done.settle()

            def normalise(b, h):
                xs, zs, ns = [a[:, GT * h:GT * (h + 1), :] for a in (x1, z, n_rows)]
                dve.wait_ge(scales_ready, 6 * b + h + 1)
                for t in range(GT):
                    done.tick(dve.tensor_scalar(zs[:, t, :], xs[:, t, :], mean_var[:, t, 0:1], r1[:, t:t + 1], ALU.subtract, ALU.mult))
                centred(ns, xs)
                for t in range(GT):
                    done.tick(dve.scalar_tensor_tensor(ns[:, t, :], ns[:, t, :], rr[:, t:t + 1], b_row[:, :], ALU.mult, ALU.add))
                done.settle()
                dve.sem_inc(rows_ready, 1)

            def residual(b, h):
                dve.wait_ge(scales_ready, 6 * b + (S_T0, S_T1)[h] + 1)
                centred(t_rows, t_rows)
                dve.wait_ge(sums_ready, 2 * b + h + 1)
                for t in range(GT):
                    done.tick(dve.scalar_tensor_tensor(t_rows[:, t, :], t_rows[:, t, :], r1[:, t:t + 1], z[:, GT * h + t, :], ALU.mult, ALU.add))
                done.settle_alone()
                statistics(t_rows)

            def m_rows(b, h):
                dve.wait_ge(scales_ready, 6 * b + (S_M0, S_M1)[h] + 1)
                centred(t_rows, t_rows)
                for t in range(GT):
                    done.tick(dve.scalar_tensor_tensor(t_rows[:, t, :], t_rows[:, t, :], r1[:, t:t + 1], b_row[:, :], ALU.mult, ALU.add))
                done.settle()
                dve.sem_inc(rows_ready, 1)

            def rest(b, m, h, c):
                n = chunk0[m, h] + c
                dve.wait_ge(ring_free, USES * b + use0[m, h] + c + RING + 1)
                dve.tensor_tensor(hid[n % PARTS][1][:, :], gelu[n % GELUS][:, :], hid[n % PARTS][0][:, :].bitcast(fp32), ALU.subtract).then_inc(hid_ready, 1)

            def project(b, m, h):
                dve.wait_ge(hid_used, CHUNKS * b + chunk0[m, h] + FC + PARTS)
                for k in range(KD):
                    last = dve.tensor_scalar(proj_t[m][:, k, GW * h:GW * (h + 1)], acc[k][:, :], b2[:, m, k:k + 1], None, ALU.add)
                    done.tick(last)
                done.settle()
                dve.sem_inc(acc_free, 1)

            def turned_rest(b, order, h):
                dve.wait_ge(hi_ready, 4 * b + order + 1)
                for k in range(KD):
                    done.tick(dve.tensor_tensor(rows_t[h][1][:, k, :], work[k][:, :], rows_t[h][0][:, k, :].bitcast(fp32), ALU.subtract))
                done.settle()
                dve.sem_inc(work_free, 1)
                dve.sem_inc(turned_ready, 1)

            def add_out(b, h):
                dve.wait_ge(hid_used, CHUNKS * b + chunk0[FM, h] + FC + PARTS)
                for j in range(2):
                    xs = x1[:, GT * h + 2 * j:GT * h + 2 * j + 2, :]
                    done.tick(dve.tensor_tensor(xs, xs, acc[j][:, :].rearrange("p (t d) -> p t d", t=2), ALU.add))
                done.settle()
                dve.sem_inc(acc_free, 1)
                dve.sem_inc(out_ready, 1)

            def sequence(b, more):
                for c in range(FC):
                    rest(b, H1, 0, c)
                    if c == 3:
                        add_rows(b, 1)
                    if c == 5:
                        statistics(x1[:, GT:2 * GT, :])
                project(b, H1, 0)
                for c in range(FC):
                    rest(b, H2, 0, c)
                    if c == 1:
                        normalise(b, 1)
                project(b, H2, 0)
                turned_rest(b, R_N1, 1)
                for c in range(FC):
                    rest(b, H1, 1, c)
                    if c == 1:
                        dve.wait_ge(work_free, 6 * b + W_T0 + 3)
                        statistics(t_rows)
                    if c == 3:
                        residual(b, 0)
                    if c == 6:
                        m_rows(b, 0)
                project(b, H1, 1)
                for c in range(FC):
                    rest(b, H2, 1, c)
                project(b, H2, 1)
                turned_rest(b, R_M0, 0)
                for c in range(FC):
                    rest(b, FM, 0, c)
                    if c == 0:
                        dve.wait_ge(work_free, 6 * b + W_T1 + 3)
                        statistics(t_rows)
                    if c == 2:
                        residual(b, 1)
                    if c == 4:
                        m_rows(b, 1)
                add_out(b, 0)
                turned_rest(b, R_M1, 1)
                for c in range(FC):
                    if c == FC - 1 and more:
                        turned_rest(b + 1, R_N0, 0)
                    rest(b, FM, 1, c)
                    if more:
                        if c == 0:
                            add_rows(b + 1, 0)
                        if c == 2:
                            statistics(x1[:, 0:GT, :])
                        if c == 4:
                            normalise(b + 1, 0)
                add_out(b, 1)

            done.enter(0, 9 + 8 + 12 + 2)
            add_rows(0, 0)
            statistics(x1[:, 0:GT, :])
            normalise(0, 0)
            turned_rest(0, R_N0, 0)
            done.leave(1)
            with dve.Fori(0, SEQS - 1) as b:
                done.enter(b, 142)
                sequence(b, True)
                done.leave(SEQS - 1)
            done.enter(0, 111)
            sequence(SEQS - 1, False)
            done.leave(1)

        @block.tensor
        def _(pe):
            pe.sem_inc(hid_used, PARTS)
            pe.wait_ge(w_split, 6)
            TERMS = ((0, 0), (1, 0), (0, 1))

            def turn(b, order, v, src):
                pe.wait_ge(rows_ready, 4 * b + order + 1)
                pe.wait_ge(work_free, 6 * b + v + 2)
                for k in range(KD):
                    for t in range(GT):
                        last = pe.transpose(work[k][:, t * P:(t + 1) * P], src[:, t, k * P:(k + 1) * P], consts["eye"][:, :])
                last.then_inc(work_full, 1)

            def up(b, m, h, c):
                use = use0[m, h] + c
                pe.wait_ge(ring_free, USES * b + use + 1)
                n = 0
                for k in range(KD):
                    for wp, xp in TERMS:
                        last = pe.matmul(ring[use % RING][:, :], w1[m][wp][:, k, c * P:(c + 1) * P], rows_t[h][xp][:, k, :], start=(n == 0), stop=(n == 2 * len(TERMS) - 1))
                        n += 1
                last.then_inc(ring_full, 1)

            def down(b, m, h, c):
                j = (chunk0[m, h] + c) % PARTS
                if c == 0:
                    pe.wait_ge(acc_free, 6 * b + group0[m, h] + 1)
                pe.wait_ge(hid_ready, CHUNKS * b + chunk0[m, h] + c + GELUS + 1)
                if m == FM:
                    for t in range(GT):
                        for q, (wp, xp) in enumerate(TERMS):
                            last = pe.matmul(acc[t // 2][:, (t % 2) * D:(t % 2 + 1) * D], hid[j][xp][:, t * P:(t + 1) * P], w2[m][wp][:, c, :],
                                             start=(c == 0 and q == 0 and t % 2 == 0), stop=(c == FC - 1 and q == 2), skip_group_check=True)
                else:
                    for k in range(KD):
                        for q, (wp, xp) in enumerate(TERMS):
                            last = pe.matmul(acc[k][:, :], w2[m][wp][:, c, k * P:(k + 1) * P], hid[j][xp][:, :], start=(c == 0 and q == 0), stop=(c == FC - 1 and q == 2))
                last.then_inc(hid_used, 1)

            def mlp(b, m, h, more=False):
                for c in range(FC):
                    if c == FC - 1 and more:
                        turn(b + 1, R_N0, W_N0_NEXT - 6, n_rows[:, 0:GT, :])
                    if c == 0:
                        pe.wait_ge(turned_ready, 4 * b + {(H1, 0): R_N0, (H2, 0): R_N0, (H1, 1): R_N1, (H2, 1): R_N1, (FM, 0): R_M0, (FM, 1): R_M1}[m, h] + 1)
                    up(b, m, h, c)
                    if c >= LAG:
                        down(b, m, h, c - LAG)
                for c in range(FC - LAG, FC):
                    down(b, m, h, c)

            def score_tiles(b, h):
                for i in range(GT * (h + 1)):
                    lo = max(i - GT * h, 0) * P
                    use = use0[f"scores{h}"] + i
                    pe.wait_ge(ring_free, USES * b + use + 1)
                    if i % GT == 0:
                        pe.wait_ge(acc_free, 6 * b + (group0[H2, i // GT] if i // GT == h else group0[H1, h]) + 2)
                    for k in range(KD):
                        last = pe.matmul(ring[use % RING][:, lo:GW], proj_t[1][:, k, i * P:(i + 1) * P], proj_t[0][:, k, GW * h + lo:GW * (h + 1)], start=(k == 0), stop=(k == KD - 1))
                    last.then_inc(ring_full, 1)

            def t_tiles(b, h, v):
                pe.wait_ge(work_free, 6 * b + v + 2)
                for d in range(GT):
                    pe.wait_ge(ring_free, USES * b + use0[f"scores{h}"] + GT * h + d + 1 + RING)
                    pe.wait_ge(masked, 8 * b + GT * h + d + 1)
                    for i in range(GT * h + d + 1):
                        last = pe.matmul(work[d // 2][:, (d % 2) * D:(d % 2 + 1) * D], score_tile(i, d * P, (d + 1) * P), n_rows[:, i, :], start=(i == 0), stop=(i == GT * h + d))
                last.then_inc(work_full, 1)

            def sequence(b, more):
                mlp(b, H1, 0)
                mlp(b, H2, 0)
                score_tiles(b, 0)
                turn(b, R_N1, W_N1, n_rows[:, GT:2 * GT, :])
                t_tiles(b, 0, W_T0)
                mlp(b, H1, 1)
                mlp(b, H2, 1)
                score_tiles(b, 1)
                turn(b, R_M0, W_M0, t_rows)
                t_tiles(b, 1, W_T1)
                mlp(b, FM, 0)
                turn(b, R_M1, W_M1, t_rows)
                mlp(b, FM, 1, more)

            turn(0, R_N0, -1, n_rows[:, 0:GT, :])
            with pe.Fori(0, SEQS - 1) as b:
                sequence(b, True)
            sequence(SEQS - 1, False)


def constants(nc, ctx, outer):
    kit = Kit(nc, ctx, outer, "const")
    sb = kit.sb
    c = {
        "eye": sb("eye", [P, P]), "earlier": sb("earlier", [P, P], bf16), "ones": sb("ones", [P, P], bf16),
        "zeros": sb("zeros", [P, D], bf16), "iota_e": sb("iota_e", [P, EXPERTS], bf16),
        "iota_c": sb("iota_c", [P, CAP], bf16), "partition": sb("partition", [P, 1]), "tile": sb("tile", [P, TILES]),
        "minus_half": sb("minus_half", [P, 2 * GT]),
    }
    c["passed"] = kit.sem("passed")
    filled = kit.sem("filled")
    with ExitStack() as own:
        block = own.enter_context(nc.Block())

        @block.gpsimd
        def _(pool):
            fills = [("eye", 0.0), ("earlier", 1.0), ("ones", 1.0), ("zeros", 0.0), ("minus_half", -0.5)]
            for name, value in fills:
                pool.memset(c[name][:, :], value).then_inc(filled, 1)
            pool.wait_ge(filled, len(fills))
            pool.affine_select(out=c["eye"][:, :], in_=c["eye"][:, :], compare_op=ALU.not_equal, fill=1.0,
                               base=0, pattern=[[-1, P]], channel_multiplier=1).then_inc(filled, 1)
            pool.affine_select(out=c["earlier"][:, :], in_=c["earlier"][:, :], compare_op=ALU.is_gt, fill=0.0,
                               base=0, pattern=[[1, P]], channel_multiplier=-1).then_inc(filled, 1)
            for name, step, n, mult in (("iota_e", 1, EXPERTS, 0), ("iota_c", 1, CAP, 0), ("partition", 1, 1, 1), ("tile", 1, TILES, 0)):
                pool.iota(c[name][:, :], pattern=[[step, n]], base=0, channel_multiplier=mult,
                          allow_small_or_imprecise_dtypes=True).then_inc(filled, 1)
            pool.wait_ge(filled, len(fills) + 6)
    return c


def build(nc, x, w, aw, out):
    with ExitStack() as outer, ExitStack() as ctx:
        xn_d = nc.dram_tensor("xn_rows", (TOKENS, D), fp32, kind="Internal").ap()
        base_d = nc.dram_tensor("base_rows", (TOKENS, D), fp32, kind="Internal").ap()
        y_d = nc.dram_tensor("expert_rows", (SLOTS + 1, D), fp32, kind="Internal").ap()
        consts = constants(nc, ctx, outer)
        kit = Kit(nc, ctx, outer, "routing")
        routing = {"lists": kit.sb("lists", [P, EXPERTS, CH], u32), "slots": kit.sb("slots", [P, TILES, 2], u32),
                   "halves": kit.sb("halves", [P, TILES, 2])}
        x_rows = x.rearrange("b s d -> (b s) d")
        out_rows = out.rearrange("b s d -> (b s) d")
        dispatch(nc, outer, "dispatch0", consts, routing, x_rows, w, xn_d, base_d)
        experts(nc, outer, "experts0", consts, routing, w, xn_d, y_d)
        x2_d = nc.dram_tensor("x2_rows", (TOKENS, D), fp32, kind="Internal").ap()
        attention(nc, outer, "attention", consts, routing, aw, base_d, y_d, x2_d)
        dispatch(nc, outer, "dispatch1", consts, routing, x2_d, w, xn_d, base_d)
        experts(nc, outer, "experts1", consts, routing, w, xn_d, y_d)
        combine(nc, outer, "combine", consts, routing, base_d, y_d, out_rows)


_FFN = ["rms_w", "gate_w", "w13", "w2", "sw_gate", "sw_up", "sw_down"]
_ATTN = ["x", "ln_g", "ln_b"] + [f"{m}_{p}" for m in ("h1", "h2", "fm") for p in ("w1", "b1", "w2", "b2")]


def kernel(**inputs):
    import concourse.bacc as _bacc
    from concourse.bass_utils import run_bass_kernel_spmd as _run

    nc = _bacc.Bacc("TRN2", target_bir_lowering=False, num_devices=1)
    arrays = {}

    def declare(prefix, names):
        aps = {}
        for name in names:
            a = np.ascontiguousarray(inputs[prefix + name])
            arrays[f"in_{prefix}{name}"] = a
            aps[name] = nc.dram_tensor(f"in_{prefix}{name}", a.shape, mybir.dt.from_np(a.dtype), kind="ExternalInput").ap()
        return aps

    aw, w = declare("L0_attn_", _ATTN), declare("L0_ffn_", _FFN)
    out = nc.dram_tensor("out", (SEQS, SEQ, D), fp32, kind="ExternalOutput").ap()
    build(nc, aw["x"], w, aw, out)
    r = _run(nc, [arrays], core_ids=[0])
    return r.results[0]["out"]
```
